# Optimizing a Trainium2 kernel written in Bass

```python
import numpy as np
import jax
import jax.numpy as jnp

def _softmax(x, axis=-1):
    return jax.nn.softmax(x, axis=axis)

def _gelu(x):
    return jax.nn.gelu(x, approximate=True)

def _silu(x):
    return jax.nn.silu(x)

def _sigmoid(x):
    return jax.nn.sigmoid(x)

def _layernorm(x, axis=-1, eps=1e-05):
    m = jnp.mean(x, axis=axis, keepdims=True)
    v = jnp.var(x, axis=axis, keepdims=True)
    return (x - m) / jnp.sqrt(v + eps)

def _scatter_add(tgt, idx, src, axis=0):
    return tgt.at[idx].add(src)

def _segment_sum(src, seg, n):
    return jax.ops.segment_sum(src, seg, n)
kernel_name = 'mk_prb_d2_jaxref_r8_39d868'

def setup_inputs(seed: int=0):
    np.random.seed(seed)
    _w = jnp.asarray

    def _L0_attn_setup():
        import jax, jax.numpy as jnp
        import numpy as np
        B, T, HID = (4, 256, 128)
        NH = 4
        KD, VD = (64, 128)
        DK, DV = (KD // NH, VD // NH)
        R = 32
        GLR = 64
        EPS = 1e-05

        def _rwkv6_scan(r, k, v, w, u):

            def step(S, xs):
                r_t, k_t, v_t, w_t = xs
                kv = k_t[..., :, None] * v_t[..., None, :]
                o_t = jnp.einsum('bhk,bhkv->bhv', r_t, S + u[None, :, :, None] * kv)
                S = jnp.exp(w_t)[..., None] * S + kv
                return (S, o_t)
            S0 = jnp.zeros(r.shape[:2] + (r.shape[-1], v.shape[-1]), r.dtype)
            mv = lambda x: jnp.moveaxis(x, 2, 0)
            _, o = jax.lax.scan(step, S0, (mv(r), mv(k), mv(v), mv(w)))
            return jnp.moveaxis(o, 0, 2)
        key = jax.random.key(seed)
        ks = jax.random.split(key, 20)
        g = lambda i, shape, s=0.02: jax.random.normal(ks[i], shape, dtype=jnp.float32) * s
        return {'hidden_states': jax.random.normal(ks[0], (B, T, HID), dtype=jnp.float32), 'mu0': g(1, (HID,), 0.1), 'W_x0': g(2, (5 * R, HID)), 'W_x2': g(3, (HID, 5 * R)), 'x_bias': g(4, (5, HID), 0.1), 'W_r': g(5, (KD, HID)), 'W_w1': g(6, (GLR, HID)), 'W_w2': g(7, (KD, GLR)), 'b_w2': g(8, (KD,), 0.1), 'W_k': g(9, (KD, HID)), 'W_v': g(10, (VD, HID)), 'W_g': g(11, (VD, HID)), 'bonus': g(12, (NH, DK), 0.1), 'gn_weight': jnp.ones((VD,), jnp.float32) + g(13, (VD,), 0.05), 'gn_bias': g(14, (VD,), 0.05), 'W_o': g(15, (HID, VD))}
    _L0_attn_in = _L0_attn_setup()

    def _L0_ffn_setup():
        import jax, jax.numpy as jnp
        import numpy as np
        BS, L, D = (4, 256, 128)
        H, E, K = (8, 16, 2)
        HD = D // H
        I = 512 // H
        key = jax.random.key(seed)
        ks = jax.random.split(key, 10)
        s = lambda k, shp, fan: jax.random.normal(k, shp, jnp.float32) / np.sqrt(fan)
        return {'x': jax.random.normal(ks[0], (BS, L, D), jnp.float32), 'Wm': s(ks[1], (D, D), D), 'bm': jnp.zeros((D,), jnp.float32), 'expert_emb': jax.random.normal(ks[2], (HD, E), jnp.float32), 'W1': s(ks[3], (E, HD, I), HD), 'b1': jnp.zeros((E, I), jnp.float32), 'W2': s(ks[4], (E, I, HD), I), 'b2': jnp.zeros((E, HD), jnp.float32), 'Wo': s(ks[5], (D, D), D), 'bo': jnp.zeros((D,), jnp.float32)}
    _L0_ffn_in = _L0_ffn_setup()

    def _L1_attn_setup():
        import jax, jax.numpy as jnp
        import numpy as np
        N_EMBD = 128
        N_HEAD = 16
        HEAD_DIM = N_EMBD // N_HEAD
        LATENT_DIM = N_EMBD // 2
        B, T = (4, 256)
        key = jax.random.key(seed)
        ks = jax.random.split(key, 5)

        def init(k, fan_in, fan_out):
            bound = 1.0 / np.sqrt(fan_in)
            return jax.random.uniform(k, (fan_in, fan_out), jnp.float32, -bound, bound)
        return {'x': jax.random.normal(ks[0], (B, T, N_EMBD), jnp.float32), 'Wc_down': init(ks[1], N_EMBD, LATENT_DIM), 'Wq_up': init(ks[2], LATENT_DIM, N_EMBD), 'Wkv_up': init(ks[3], LATENT_DIM, 2 * HEAD_DIM), 'Wc_proj': init(ks[4], N_EMBD, N_EMBD)}
    _L1_attn_in = _L1_attn_setup()

    def _L1_ffn_setup():
        import jax, jax.numpy as jnp
        import numpy as np
        EPS = 1e-09
        RMS_EPS = 1e-06
        TOP_K = 2
        LOOPS = 2

        def _rmsnorm(x, w):
            var = jnp.mean(x * x, axis=-1, keepdims=True)
            return x * jax.lax.rsqrt(var + RMS_EPS) * w

        def _swiglu(x, w1, w3, w2):
            h = jax.nn.silu(x @ w1) * (x @ w3)
            return h @ w2
        key = jax.random.key(seed)
        ks = jax.random.split(key, 5)
        B, S, D, F, E = (4, 256, 128, 256, 8)
        z = jax.random.normal(ks[0], (B, S, D), dtype=jnp.float32)
        norm_w = jnp.ones((D,), dtype=jnp.float32)
        router_w = jax.random.normal(ks[1], (D, E), dtype=jnp.float32) * 0.02
        w1 = jax.random.normal(ks[2], (E, D, F), dtype=jnp.float32) * 0.02
        w3 = jax.random.normal(ks[3], (E, D, F), dtype=jnp.float32) * 0.02
        w2 = jax.random.normal(ks[4], (E, F, D), dtype=jnp.float32) * 0.02
        return {'z': z, 'norm_w': norm_w, 'router_w': router_w, 'w1': w1, 'w3': w3, 'w2': w2}
    _L1_ffn_in = _L1_ffn_setup()
    _d = {'L0_attn_hidden_states': _L0_attn_in['hidden_states'], 'L0_attn_mu0': _L0_attn_in['mu0'], 'L0_attn_W_x0': _L0_attn_in['W_x0'], 'L0_attn_W_x2': _L0_attn_in['W_x2'], 'L0_attn_x_bias': _L0_attn_in['x_bias'], 'L0_attn_W_r': _L0_attn_in['W_r'], 'L0_attn_W_w1': _L0_attn_in['W_w1'], 'L0_attn_W_w2': _L0_attn_in['W_w2'], 'L0_attn_b_w2': _L0_attn_in['b_w2'], 'L0_attn_W_k': _L0_attn_in['W_k'], 'L0_attn_W_v': _L0_attn_in['W_v'], 'L0_attn_W_g': _L0_attn_in['W_g'], 'L0_attn_bonus': _L0_attn_in['bonus'], 'L0_attn_gn_weight': _L0_attn_in['gn_weight'], 'L0_attn_gn_bias': _L0_attn_in['gn_bias'], 'L0_attn_W_o': _L0_attn_in['W_o'], 'L0_ffn_Wm': _L0_ffn_in['Wm'], 'L0_ffn_bm': _L0_ffn_in['bm'], 'L0_ffn_expert_emb': _L0_ffn_in['expert_emb'], 'L0_ffn_W1': _L0_ffn_in['W1'], 'L0_ffn_b1': _L0_ffn_in['b1'], 'L0_ffn_W2': _L0_ffn_in['W2'], 'L0_ffn_b2': _L0_ffn_in['b2'], 'L0_ffn_Wo': _L0_ffn_in['Wo'], 'L0_ffn_bo': _L0_ffn_in['bo'], 'L1_attn_Wc_down': _L1_attn_in['Wc_down'], 'L1_attn_Wq_up': _L1_attn_in['Wq_up'], 'L1_attn_Wkv_up': _L1_attn_in['Wkv_up'], 'L1_attn_Wc_proj': _L1_attn_in['Wc_proj'], 'L1_ffn_norm_w': _L1_ffn_in['norm_w'], 'L1_ffn_router_w': _L1_ffn_in['router_w'], 'L1_ffn_w1': _L1_ffn_in['w1'], 'L1_ffn_w3': _L1_ffn_in['w3'], 'L1_ffn_w2': _L1_ffn_in['w2']}
    _x0 = _d['L0_attn_hidden_states']
    _d['L0_attn_hidden_states'] = jax.random.normal(jax.random.fold_in(jax.random.key(seed), 1), (4, 1024, 128), dtype=_x0.dtype)
    del _x0
    return _d

def reference(L0_attn_hidden_states, L0_attn_mu0, L0_attn_W_x0, L0_attn_W_x2, L0_attn_x_bias, L0_attn_W_r, L0_attn_W_w1, L0_attn_W_w2, L0_attn_b_w2, L0_attn_W_k, L0_attn_W_v, L0_attn_W_g, L0_attn_bonus, L0_attn_gn_weight, L0_attn_gn_bias, L0_attn_W_o, L0_ffn_Wm, L0_ffn_bm, L0_ffn_expert_emb, L0_ffn_W1, L0_ffn_b1, L0_ffn_W2, L0_ffn_b2, L0_ffn_Wo, L0_ffn_bo, L1_attn_Wc_down, L1_attn_Wq_up, L1_attn_Wkv_up, L1_attn_Wc_proj, L1_ffn_norm_w, L1_ffn_router_w, L1_ffn_w1, L1_ffn_w3, L1_ffn_w2):

    def _L0_attn_ref(hidden_states, mu0, W_x0, W_x2, x_bias, W_r, W_w1, W_w2, b_w2, W_k, W_v, W_g, bonus, gn_weight, gn_bias, W_o):
        import jax, jax.numpy as jnp
        import numpy as np
        B, T, HID = (4, 256, 128)
        NH = 4
        KD, VD = (64, 128)
        DK, DV = (KD // NH, VD // NH)
        R = 32
        GLR = 64
        EPS = 1e-05

        def _rwkv6_scan(r, k, v, w, u):

            def step(S, xs):
                r_t, k_t, v_t, w_t = xs
                kv = k_t[..., :, None] * v_t[..., None, :]
                o_t = jnp.einsum('bhk,bhkv->bhv', r_t, S + u[None, :, :, None] * kv)
                S = jnp.exp(w_t)[..., None] * S + kv
                return (S, o_t)
            S0 = jnp.zeros(r.shape[:2] + (r.shape[-1], v.shape[-1]), r.dtype)
            mv = lambda x: jnp.moveaxis(x, 2, 0)
            _, o = jax.lax.scan(step, S0, (mv(r), mv(k), mv(v), mv(w)))
            return jnp.moveaxis(o, 0, 2)
        x = hidden_states
        shifted = jnp.pad(x, ((0, 0), (1, 0), (0, 0)))[:, :-1]
        delta = shifted - x
        xp = jnp.tanh((x + delta * mu0) @ W_x0.T)
        xp = xp.reshape(x.shape[0], x.shape[1], 5, R)
        mus = jnp.einsum('blnr,hnr->blnh', xp, W_x2.reshape(HID, 5, R)) + x_bias
        mu_r, mu_w, mu_k, mu_v, mu_g = (mus[:, :, i] for i in range(5))
        r = (x + delta * mu_r) @ W_r.T
        w = jnp.tanh((x + delta * mu_w) @ W_w1.T) @ W_w2.T + b_w2
        k = (x + delta * mu_k) @ W_k.T
        v = (x + delta * mu_v) @ W_v.T
        g = (x + delta * mu_g) @ W_g.T
        split = lambda t, d: t.reshape(t.shape[0], t.shape[1], NH, d).transpose(0, 2, 1, 3)
        r_, k_, w_ = (split(r, DK), split(k, DK), split(w, DK))
        v_ = split(v, DV)
        w_ = -jnp.exp(w_)
        o = _rwkv6_scan(r_, k_, v_, w_, bonus)
        o = o.transpose(0, 2, 1, 3)
        mean = o.mean(-1, keepdims=True)
        var = o.var(-1, keepdims=True)
        o = (o - mean) * jax.lax.rsqrt(var + EPS)
        o = o.reshape(x.shape[0], x.shape[1], VD) * gn_weight + gn_bias
        o = o * jax.nn.silu(g)
        return o @ W_o.T

    def _L0_ffn_ref(x, Wm, bm, expert_emb, W1, b1, W2, b2, Wo, bo):
        import jax, jax.numpy as jnp
        import numpy as np
        BS, L, D = (4, 256, 128)
        H, E, K = (8, 16, 2)
        HD = D // H
        I = 512 // H
        bs, L_, d = x.shape
        h = x @ Wm + bm
        t = h.reshape(bs * L_ * H, HD)
        logits = t @ expert_emb
        w = jax.nn.softmax(logits, axis=-1)
        topw, topi = jax.lax.top_k(w, K)
        hmid = jax.nn.gelu(jnp.einsum('td,edi->tei', t, W1) + b1, approximate=False)
        eo = jnp.einsum('tei,eio->teo', hmid, W2) + b2
        sel = jnp.take_along_axis(eo, topi[:, :, None], axis=1)
        comb = (sel * topw[:, :, None]).sum(axis=1)
        out = comb.reshape(bs, L_, d)
        return out @ Wo + bo

    def _L1_attn_ref(x, Wc_down, Wq_up, Wkv_up, Wc_proj):
        import jax, jax.numpy as jnp
        import numpy as np
        N_EMBD = 128
        N_HEAD = 16
        HEAD_DIM = N_EMBD // N_HEAD
        LATENT_DIM = N_EMBD // 2
        B, T = (4, 256)
        Bsz, Tlen, C = x.shape
        latent = x @ Wc_down
        q = (latent @ Wq_up).reshape(Bsz, Tlen, N_HEAD, HEAD_DIM)
        kv = latent @ Wkv_up
        k, v = (kv[..., :HEAD_DIM], kv[..., HEAD_DIM:])
        scale = 1.0 / np.sqrt(HEAD_DIM)
        att = jnp.einsum('bthd,bsd->bhts', q, k) * scale
        causal = jnp.tril(jnp.ones((Tlen, Tlen), dtype=bool))
        att = jnp.where(causal[None, None], att, -jnp.inf)
        att = jax.nn.softmax(att, axis=-1)
        y = jnp.einsum('bhts,bsd->bthd', att, v).reshape(Bsz, Tlen, C)
        return y @ Wc_proj

    def _L1_ffn_ref(z, norm_w, router_w, w1, w3, w2):
        import jax, jax.numpy as jnp
        import numpy as np
        EPS = 1e-09
        RMS_EPS = 1e-06
        TOP_K = 2
        LOOPS = 2

        def _rmsnorm(x, w):
            var = jnp.mean(x * x, axis=-1, keepdims=True)
            return x * jax.lax.rsqrt(var + RMS_EPS) * w

        def _swiglu(x, w1, w3, w2):
            h = jax.nn.silu(x @ w1) * (x @ w3)
            return h @ w2
        B, S, D = z.shape
        E = router_w.shape[-1]
        T = B * S
        for _ in range(LOOPS):
            z_norm = _rmsnorm(z, norm_w)
            logits = z_norm @ router_w
            scores = jax.nn.softmax(logits, axis=-1)
            topk_vals, topk_idx = jax.lax.top_k(scores, TOP_K)
            topk_vals = topk_vals / (jnp.sum(topk_vals, axis=-1, keepdims=True) + EPS)
            cw = jnp.sum(jax.nn.one_hot(topk_idx, E, dtype=z.dtype) * topk_vals[..., None], axis=-2)
            flat_z = z_norm.reshape(T, D)
            flat_cw = cw.reshape(T, E)
            mixed = jnp.zeros((T, D), dtype=z.dtype)
            for e in range(E):
                mixed = mixed + flat_cw[:, e:e + 1] * _swiglu(flat_z, w1[e], w3[e], w2[e])
            z = z + mixed.reshape(B, S, D)
        return z
    x = L0_attn_hidden_states
    xn = _layernorm(x, axis=-1)
    x = x + _L0_attn_ref(xn, L0_attn_mu0, L0_attn_W_x0, L0_attn_W_x2, L0_attn_x_bias, L0_attn_W_r, L0_attn_W_w1, L0_attn_W_w2, L0_attn_b_w2, L0_attn_W_k, L0_attn_W_v, L0_attn_W_g, L0_attn_bonus, L0_attn_gn_weight, L0_attn_gn_bias, L0_attn_W_o) + _L0_ffn_ref(xn, L0_ffn_Wm, L0_ffn_bm, L0_ffn_expert_emb, L0_ffn_W1, L0_ffn_b1, L0_ffn_W2, L0_ffn_b2, L0_ffn_Wo, L0_ffn_bo)
    xn = _layernorm(x, axis=-1)
    x = x + _L1_attn_ref(xn, L1_attn_Wc_down, L1_attn_Wq_up, L1_attn_Wkv_up, L1_attn_Wc_proj) + _L1_ffn_ref(xn, L1_ffn_norm_w, L1_ffn_router_w, L1_ffn_w1, L1_ffn_w3, L1_ffn_w2)
    return x

_drawn_inputs = setup_inputs


def setup_inputs(seed=0):
    import zlib

    import numpy as np

    out = dict(_drawn_inputs(seed))
    spreads = {'L0_ffn_bm': (0.0, 0.1),
     'L0_ffn_b1': (0.0, 0.1),
     'L0_ffn_b2': (0.0, 0.1),
     'L0_ffn_bo': (0.0, 0.1),
     'L1_ffn_norm_w': (1.0, 0.6)}
    factors = {'L0_attn_mu0': 8.0,
     'L0_attn_W_x0': 8.0,
     'L0_attn_W_x2': 8.0,
     'L0_attn_x_bias': 6.771,
     'L0_attn_W_w1': 8.0,
     'L0_attn_W_w2': 8.0,
     'L0_attn_b_w2': 8.0,
     'L0_attn_bonus': 8.0,
     'L0_attn_gn_weight': 8.0,
     'L0_attn_gn_bias': 8.0,
     'L1_attn_Wc_down': 3.783,
     'L1_attn_Wq_up': 8.0,
     'L1_attn_Wkv_up': 3.589,
     'L1_attn_Wc_proj': 3.431,
     'L1_ffn_router_w': 8.0,
     'L1_ffn_w1': 8.0,
     'L1_ffn_w3': 8.0,
     'L1_ffn_w2': 8.0}
    for name, (base, spread) in spreads.items():
        noise = np.random.default_rng([zlib.crc32(name.encode()), seed]).standard_normal(out[name].shape)
        drawn = base * np.exp(spread * noise) if base else spread * noise
        out[name] = jnp.asarray(drawn.astype(out[name].dtype))
    for name, factor in factors.items():
        out[name] = (out[name] * factor).astype(out[name].dtype)
    return out
```

```python
from contextlib import ExitStack

import concourse.bass as bass
from concourse import mybir

F32 = mybir.dt.float32
BF16 = mybir.dt.bfloat16
U32 = mybir.dt.uint32
ALU = mybir.AluOpType
ACT = mybir.ActivationFunctionType
AX = mybir.AxisListType.X


class Lane:

    def __init__(self, k, engine, name, turn, turns):
        self.k, self.engine, self.turn, self.turns, self.pos = k, engine, turn, turns, 0
        self.name = name
        self.key = name.rsplit("_", 1)[1]
        self.sem = k.sem(name)
        self.per = k.counts.get(name, 1)
        self.waited = {}

    def __call__(self, instruction, name=None):
        instruction.then_inc(self.sem, 1)
        self.pos += 1
        if name:
            self.k.seen[self.name, name] = self.pos
        return (self, self.pos)

    def last(self, name):
        return (self, self.k.counts.get((self.name, name), 1) - self.per)


def wait(engine, *marks):
    latest = {}
    for lane, pos in (*marks, *owed.pop(id(engine), ())):
        latest[lane] = max(pos, latest.get(lane, pos))
    due = []
    for lane, pos in latest.items():
        if pos > lane.waited.get(id(engine), -lane.per):
            lane.waited[id(engine)] = pos
            due.append((lane.sem, lane.turn * lane.per + (lane.per + pos)))
    for sem, value in due:
        engine.wait_ge(sem, value)


owed = {}


class Stage:

    def __init__(self, k, name, turns):
        self.k, self.name, self.turns = k, name, turns
        nc = k.nc
        self.engines = {"pe": nc.tensor, "dve": nc.vector, "act": nc.scalar, "pool": nc.gpsimd, "sp": nc.sync}

    def __enter__(self):
        nc = self.k.nc
        self.lanes = {e: Lane(self.k, eng, f"{self.name}_{e}", 0, self.turns) for e, eng in self.engines.items()}
        for lane in self.lanes.values():
            lane.engine.sem_inc(lane.sem, lane.per)
        self.loop = nc.Fori(0, self.turns)
        i = self.loop.__enter__()
        for lane in self.lanes.values():
            lane.turn = i
        return (i, *self.lanes.values())

    def __exit__(self, *exc):
        self.loop.__exit__(*exc)
        for lane in self.lanes.values():
            self.k.seen[lane.name] = max(lane.pos, 1)
        return False

    def over(self, *engines):
        for lane in self.lanes.values():
            if lane.pos:
                for e in engines:
                    e.wait_ge(lane.sem, (self.turns + 1) * lane.pos)


P = 128
NB, T, HID = 4, 1024, 128
N = NB * T
TILE = 512
NT = N // TILE
PITCH = TILE + 1


class Kit:

    def __init__(self, nc, ctx, counts, dram):
        self.nc, self.ctx, self.counts, self.dram, self.seen, self.drains = nc, ctx, counts, dram, {}, {}

    def sb(self, name, shape, dt=F32, ctx=None):
        return (ctx or self.ctx).enter_context(self.nc.sbuf_tensor(name, shape, dt))

    def ps(self, name, shape, ctx, dt=F32):
        return ctx.enter_context(self.nc.psum_tensor(name, shape, dt))

    def sem(self, name):
        return self.ctx.enter_context(self.nc.semaphore(name))

    def drain_sem(self, name, dmas):
        if name not in self.drains:
            self.drains[name] = (self.sem(name), dmas)
        return self.drains[name][0]

    def drained(self, engine, name, turn):
        sem, dmas = self.drains[name]
        engine.wait_ge(sem, turn * (16 * dmas) + 16 * dmas)

    def drain_over(self, name, turns):
        sem, dmas = self.drains[name]
        for e in self.all_engines():
            e.wait_ge(sem, 16 * dmas * (turns + 1))

    def all_engines(self):
        nc = self.nc
        return (nc.tensor, nc.vector, nc.scalar, nc.gpsimd, nc.sync)


def load(k, sem, total, *pairs):
    for n, (dst, src) in enumerate(pairs):
        (k.nc.sync, k.nc.scalar)[n % 2].dma_start(dst, src).then_inc(sem, 16)
        total += 16
    return total


def normalise(k, name, src, dst, ones, eps, group, centre=True, extra=None, gain=None):
    nc = k.nc
    with ExitStack() as c:
        mean = [k.ps(f"{name}_mean{g}", [P, TILE], c) for g in range(group)] if centre else None
        var = [k.ps(f"{name}_var{g}", [P, TILE], c) for g in range(group)]
        cent = [k.sb(f"{name}_cent{g}", [P, TILE], ctx=c) for g in range(group)] if centre else None
        sq = [k.sb(f"{name}_sq{g}", [P, TILE], ctx=c) for g in range(group)]
        sd = [k.sb(f"{name}_sd{g}", [P, TILE], ctx=c) for g in range(group)]
        stage = Stage(k, name, NT // group)
        with stage as (i, pe, dve, act, pool, sp):
            centred = [None] * group
            if centre:
                for g in range(group):
                    wait(nc.tensor, dve.last(f"cent{g}"))
                    got = pe(nc.tensor.matmul(mean[g][:, :], ones[:, :], src(i * group + g), start=True, stop=True))
                    wait(nc.vector, got, act.last(f"sq{g}"), dve.last(f"out{g}"))
                    centred[g] = dve(nc.vector.tensor_tensor(cent[g][:, :], src(i * group + g), mean[g][:, :], ALU.subtract), f"cent{g}")
            for g in range(group):
                if centre:
                    wait(nc.scalar, centred[g])
                wait(nc.scalar, pe.last(f"var{g}"))
                squared = act(nc.scalar.activation(sq[g][:, :], cent[g][:, :] if centre else src(i * group + g), ACT.Square), f"sq{g}")
                wait(nc.tensor, squared, act.last(f"sd{g}"))
                got = pe(nc.tensor.matmul(var[g][:, :], ones[:, :], sq[g][:, :], start=True, stop=True), f"var{g}")
            for g in range(group):
                wait(nc.scalar, (pe, pe.pos - group + 1 + g), dve.last(f"out{g}"))
                rooted = act(nc.scalar.activation(sd[g][:, :], var[g][:, :], ACT.Sqrt, bias=eps[:, 0:1]), f"sd{g}")
                wait(nc.vector, rooted)
                inverse = dve(nc.vector.reciprocal(sd[g][:, :], sd[g][:, :]))
                wait(nc.vector, inverse)
                what = cent[g][:, :] if centre else src(i * group + g)
                if gain is None:
                    out = dve(nc.vector.tensor_tensor(dst(i * group + g), what, sd[g][:, :], ALU.mult), f"out{g}")
                else:
                    out = dve(nc.vector.scalar_tensor_tensor(dst(i * group + g), what, gain, sd[g][:, :], ALU.mult, ALU.mult), f"out{g}")
                if extra:
                    extra(i * group + g, dve, out)
        stage.over(*k.all_engines())


class Ring:

    def __init__(self, k, name, slots):
        self.k, self.name, self.slots, self.n, self.held = k, name, slots, 0, {}

    def take(self, engine, lanes):
        slot = self.n % len(self.slots)
        self.n += 1
        marks = self.held.get(slot)
        if marks is None:
            before = self.k.counts.get((self.name, slot), ())
            marks = [(lanes[name], pos - lanes[name].per) for name, pos in before]
        owed[id(engine)] = (*owed.get(id(engine), ()), *marks)
        self.held[slot] = ()
        self.slot = slot
        return self.slots[slot]

    def release(self, slot, *marks):
        self.held[slot] = marks
        self.k.seen[self.name, slot] = tuple((lane.key, pos) for lane, pos in marks)


KD, NH, DK, DV = 64, 4, 16, 32
CH = 128
NC = TILE // CH
SB = 32
NJ = TILE // SB
LOW = (1, 2, 4, 8, 16)


def recurrence(k, w, xn, out, gate):
    nc = k.nc
    V, A, E, G = nc.vector, nc.scalar, nc.tensor, nc.gpsimd
    with ExitStack() as c:
        sb = lambda name, *shape: k.sb(f"rw_{name}", [P, *shape], ctx=c)
        banks = [k.ps(f"rw_bank{n}", [P, TILE], c) for n in range(8)]
        delta = [sb(f"delta{s}", TILE) for s in range(2)]
        mixed0 = [sb(f"mixed0{s}", TILE) for s in range(2)]
        low = [[sb(f"low{s}{a}", TILE) for a in range(2)] for s in range(2)]
        mix = [sb(f"mix{n}", TILE) for n in range(4)]
        hidden = [sb(f"hidden{s}", TILE) for s in range(2)]
        tanhg = [sb(f"tanhg{s}", TILE) for s in range(2)]
        rate, key, rec = sb("rate", TILE), sb("key", TILE), sb("rec", TILE)
        val = [sb(f"val{s}", TILE) for s in range(2)]
        pre, suf = sb("pre", TILE), sb("suf", TILE)
        total = {h: sb(f"total{h}", TILE // h) for h in (2, 4, 8, 16, 32, 64, 128)}
        gr = [sb(f"gr{n}", TILE // 2) for n in range(2)]
        gl = [sb(f"gl{n}", TILE // 2) for n in range(2)]
        rr = [sb(f"rr{n}", NH * TILE // 2) for n in range(2)]
        rr0 = sb("selves", NH * TILE)
        ru = sb("ru", TILE)
        kk = [sb(f"kk{n}", TILE) for n in range(2)]
        diag = sb("diag", 2, NC, NH, SB)
        full = sb("full", 2 * NC, NH, CH)
        gp, gs = sb("gp", TILE), sb("gs", TILE)
        qs, kc, kct = sb("qs", TILE), sb("kc", TILE), sb("kct", TILE)
        decay = sb("decay", NC)
        add = sb("add", NC, CH)
        state = sb("state", NC, CH)
        carry = sb("carry", CH)
        cell = sb("cell", 1)

        def carrier(bank):
            E.matmul(bank[:, 0:1], k.bf["ident"], k.bf["ident"][:, 0:1], start=True, stop=True)

        s0 = k.sem("rw_zero")
        V.memset(full[:, :, :, :], 0.0).then_inc(s0, 1)
        V.memset(carry[:, :], 0.0).then_inc(s0, 1)
        for t in kk:
            V.memset(t[:, :], 0.0).then_inc(s0, 1)
        for e in k.all_engines():
            e.wait_ge(s0, 4)
        stage = Stage(k, "rw", NT // 2)
        with stage as (it, pe, dve, act, pool, sp):
            lanes = stage.lanes
            ring = Ring(k, "rw_ring", banks)

            def take():
                b = ring.take(E, lanes)
                return ring.slot, b

            mring = Ring(k, "rw_mix", mix)
            xt = [xn[:, bass.ds((it + 4 * s) * PITCH + 1, TILE)] for s in range(2)]
            sh = [xn[:, bass.ds((it + 4 * s) * PITCH, TILE)] for s in range(2)]
            lows = [None, None]
            for s in range(2):
                d = dve(V.tensor_tensor(delta[s][:, :], sh[s], xt[s], ALU.subtract))
                wait(V, d, pe.last(f"low{s}"))
                m = dve(V.scalar_tensor_tensor(mixed0[s][:, :], delta[s][:, :], w("mu0"), xt[s], ALU.mult, ALU.add))
                for a in range(2):
                    slot, b = take()
                    wait(E, m)
                    p = pe(E.matmul(b[:, :], w(f"wx0{a}"), mixed0[s][:, :], start=True, stop=True), f"low{s}")
                    wait(A, p, pe.last(f"mus{s}"))
                    t = act(A.activation(low[s][a][:, :], b[:, :], ACT.Tanh))
                    ring.release(slot, t)
                lows[s] = t

            def mixture(i, s):
                slot, b = take()
                wait(E, lows[s])
                p = pe(E.matmul(b[:, :], w(f"wx2{i}"), low[s][i // 4][:, :], start=True, stop=True), f"mus{s}")
                m = mring.take(V, lanes)
                mslot = mring.slot
                wait(V, p)
                d = dve(V.scalar_tensor_tensor(m[:, :], b[:, :], w("xbias", i, i + 1), delta[s][:, :], ALU.add, ALU.mult))
                ring.release(slot, d)
                wait(V, d)
                d = dve(V.tensor_tensor(m[:, :], m[:, :], xt[s], ALU.add))
                return mslot, m, d

            hs = [None, None]
            for s in range(2):
                ms, m, d = mixture(1, s)
                slot, b = take()
                wait(E, d)
                p = pe(E.matmul(b[:, :], w("ww1"), m[:, :], start=True, stop=True))
                mring.release(ms, p)
                wait(A, p, pe.last(f"rate{s}"))
                hs[s] = act(A.activation(hidden[s][:, :], b[:, :], ACT.Tanh))
                ring.release(slot, hs[s])
            slot, b = take()
            for s in range(2):
                wait(E, hs[s])
                p = pe(E.matmul(b[64 * s:64 * s + KD, :], w("ww2"), hidden[s][:, :], start=True, stop=True), f"rate{s}")
            wait(A, p, dve.last("rate"))
            rated = act(A.activation(rate[:, :], b[:, :], ACT.Exp, bias=w("bw2")))
            ring.release(slot, rated)

            def project(i, weight, dst, prev):
                slot, b = take()
                p = None
                for s in range(2):
                    ms, m, d = mixture(i, s)
                    wait(E, d)
                    p = pe(E.matmul(b[64 * s:64 * s + KD, :], w(weight), m[:, :], start=True, stop=True))
                    mring.release(ms, p)
                wait(A, p, *prev)
                done = act(A.activation(dst[:, :], b[:, :], ACT.Copy))
                ring.release(slot, done)
                return done

            keyed = project(2, "wk", key, (dve.last("key"), pe.last("one")))
            recd = project(0, "wr", rec, (dve.last("rec"),))

            vals = [None, None]
            for s in range(2):
                ms, m, d = mixture(3, s)
                slot, b = take()
                wait(E, d)
                for n in range(NC):
                    p = E.matmul(b[:, n * CH:(n + 1) * CH], m[:, n * CH:(n + 1) * CH], w("wv"), start=True, stop=True)
                p = pe(p)
                mring.release(ms, p)
                wait(A, p, pe.last(f"out{s}"))
                vals[s] = act(A.activation(val[s][:, :], b[:, :], ACT.Copy))
                ring.release(slot, vals[s])
            for s in range(2):
                ms, m, d = mixture(4, s)
                slot, b = take()
                wait(E, d)
                p = pe(E.matmul(b[:, :], w("wg"), m[:, :], start=True, stop=True))
                mring.release(ms, p)
                wait(A, p, dve.last(f"gate{s}"))
                t = act(A.activation(tanhg[s][:, :], b[:, :], ACT.Tanh, scale=0.5))
                wait(V, t)
                d = dve(V.scalar_tensor_tensor(gate[:, bass.ds((it + 4 * s) * TILE, TILE)], tanhg[s][:, :], 1.0, b[:, :], ALU.add, ALU.mult), f"gate{s}")
                ring.release(slot, d)

            def halves(t, h):
                v = t[:, :].rearrange("p (n e h) -> p n e h", e=2, h=h)
                return v[:, :, 0, :], v[:, :, 1, :]

            def spread(h, odd, n, width):
                src = rate if h == 1 else total[h]
                v = src[:, :].rearrange("p (n e) -> p n e", e=2)[:, :, odd:odd + 1]
                return v.broadcast_to([P, n, width])

            wait(V, recd, keyed)
            d = dve(V.tensor_scalar(ru[:, :], rec[:, :], w("bonus"), None, ALU.mult))
            wait(V, d, pe.last("self"))
            for h in range(NH):
                src = ru[:, :].rearrange("p (j t) -> p j t", t=SB)
                dst = rr0[:, :].rearrange("p (j h t) -> p j h t", h=NH, t=SB)[:, :, h, :]
                selfr = dve(V.tensor_scalar(dst, src, w("headmask", h, h + 1), None, ALU.mult))

            def blocks(keys, recs, width, ready, name):
                got = []
                for s in range(2):
                    slot, b = take()
                    wait(E, *ready)
                    carrier(b)
                    for j in range(NJ):
                        cc, q = divmod(j, CH // SB)
                        p = E.matmul(b[SB * q:SB * q + SB, cc * NH * width:(cc + 1) * NH * width],
                                     keys[64 * s:64 * s + KD, SB * j:SB * j + SB],
                                     recs[64 * s:64 * s + KD, j * NH * width:(j + 1) * NH * width],
                                     start=True, stop=True)
                    got.append((slot, b, pe(p, name if s == 1 else None)))
                return got

            for s, (slot, b, p) in enumerate(blocks(key, rr0, SB, (selfr,), "self")):
                wait(V, p, act.last("full"), dve.last("full"))
                placed = dve(V.tensor_tensor(diag[:, s, :, :, :].rearrange("p c h t -> p (c h) t"),
                                             b[:, :].rearrange("p (n t) -> p n t", t=SB),
                                             w("eye32").unsqueeze(1).broadcast_to([P, NC * NH, SB]), ALU.mult))
                ring.release(slot, placed)

            def levels(h):
                g = h // 2
                n = TILE // h
                nonlocal summed
                if g == 1:
                    wait(V, rated)
                    pe_, po = halves(pre, 1)
                    se, so = halves(suf, 1)
                    re_, ro = halves(rate, 1)
                    wait(V, act.last("gp"))
                    V.memset(pe_, 0.0)
                    V.memset(so, 0.0)
                    V.tensor_copy(po, re_)
                    V.tensor_copy(se, ro)
                    summed = dve(V.tensor_tensor(total[2][:, :].unsqueeze(2), re_, ro, ALU.add), "rate")
                else:
                    wait(V, summed, *exps)
                    _, po = halves(pre, g)
                    se, _ = halves(suf, g)
                    dve(V.tensor_tensor(po, po, spread(g, 0, n, g), ALU.add))
                    dve(V.tensor_tensor(se, se, spread(g, 1, n, g), ALU.add))
                    tt = total[g][:, :].rearrange("p (n e) -> p n e", e=2)
                    summed = dve(V.tensor_tensor(total[h][:, :].unsqueeze(2), tt[:, :, 0:1], tt[:, :, 1:2], ALU.add))

            summed, exps = None, ()
            pending = None
            for li, h in enumerate((1, 2, 4, 8, 16, 32, 64)):
                n = TILE // (2 * h)
                par = li % 2
                R, K_ = rr[par], kk[par]
                if h > 1:
                    levels(h)
                    wait(A, summed)
                    _, po = halves(pre, h)
                    se, _ = halves(suf, h)
                    wait(A, scaled[par]) if li > 2 else wait(A, dve.last(f"scaled{par}"))
                    e1 = act(A.activation(gr[par][:, :].rearrange("p (n h) -> p n h", h=h), po, ACT.Exp, scale=-1.0))
                    e2 = act(A.activation(gl[par][:, :].rearrange("p (n h) -> p n h", h=h), se, ACT.Exp, scale=-1.0))
                    exps = (e1, e2)
                    wait(V, e1, e2)
                else:
                    scaled = [None, None]
                wait(V, read[par]) if li > 1 else wait(V, pe.last(f"read{par}"))
                if li == 0:
                    read = [None, None]
                rodd = halves(rec, h)[1]
                keven = halves(key, h)[0]
                if h <= 16:
                    rv = R[:, :].rearrange("p (j h n t) -> p j h n t", h=NH, n=16 // h, t=h)
                    dst = [rv[:, :, a, :, :] for a in range(NH)]
                    ro = rodd.rearrange("p (j n) h -> p j n h", n=16 // h)
                    gg = gr[par][:, :].rearrange("p (j n h) -> p j n h", n=16 // h, h=h)
                else:
                    rv = R[:, :].rearrange("p (j h t) -> p j h t", h=NH, t=h)
                    dst = [rv[:, :, a, :] for a in range(NH)]
                    ro, gg = rodd, gr[par][:, :].rearrange("p (n h) -> p n h", h=h)
                for a in range(NH):
                    if h == 1:
                        made = dve(V.tensor_scalar(dst[a], ro, w("headmask", a, a + 1), None, ALU.mult))
                    else:
                        made = dve(V.scalar_tensor_tensor(dst[a], gg, w("headmask", a, a + 1), ro, ALU.mult, ALU.mult))
                if h > 1:
                    ke = halves(K_, h)[0]
                    made = dve(V.tensor_tensor(ke, gl[par][:, :].rearrange("p (n h) -> p n h", h=h), keven, ALU.mult), f"scaled{par}")
                    scaled[par] = made
                if h <= 16:
                    mask = w(f"mask{h}").bitcast(U32).unsqueeze(1).broadcast_to([P, NC * NH, 16])
                    got = blocks(key if h == 1 else K_, R, 16, (made,), f"read{par}")
                    if h == 1:
                        pe_one = got[1][2]
                        k.seen["rw_pe", "one"] = pe_one[1]
                    read[par] = got[1][2]
                    for s, (slot, b, p) in enumerate(got):
                        wait(V, p, placed)
                        V.memset(cell[:, :], 0.0)
                        o = diag[:, s, :, :, :].rearrange("p c h (n e t) -> p (c h) n e t", e=2, t=h)[:, :, :, 1, :]
                        placed = dve(V.copy_predicated(o, mask.rearrange("p c (n t) -> p c n t", t=h),
                                                       b[:, 0:NC * NH * 16].rearrange("p (c n t) -> p c n t", n=16 // h, t=h)))
                        ring.release(slot, placed)
                elif h == 32:
                    for s in range(2):
                        slot, b = take()
                        wait(E, made)
                        carrier(b)
                        for n2 in range(2 * NC):
                            cc, q = divmod(n2, 2)
                            p = E.matmul(b[64 * q:64 * q + 32, cc * 128:cc * 128 + 128],
                                         K_[64 * s:64 * s + KD, 64 * n2:64 * n2 + 32],
                                         R[64 * s:64 * s + KD, n2 * 128:(n2 + 1) * 128], start=True, stop=True)
                        p = pe(p, f"read{par}")
                        wait(A, p, pe.last(f"out{s}"))
                        for q in range(2):
                            rows = slice(64 * q, 64 * q + 32)
                            d = act(A.activation(full[rows, NC * s:NC * s + NC, :, 64 * q + 32:64 * q + 64].rearrange("p c h t -> p (c h) t"),
                                                 b[rows, :].rearrange("p (n t) -> p n t", t=32), ACT.Copy))
                        ring.release(slot, d)
                    read[par] = p
                else:
                    for s in range(2):
                        for half in range(2):
                            slot, b = take()
                            wait(E, made)
                            carrier(b)
                            for n2 in range(2):
                                cc = 2 * half + n2
                                p = E.matmul(b[0:64, n2 * 256:n2 * 256 + 256],
                                             K_[64 * s:64 * s + KD, CH * cc:CH * cc + 64],
                                             R[64 * s:64 * s + KD, cc * 256:(cc + 1) * 256], start=True, stop=True)
                            p = pe(p, f"read{par}")
                            wait(A, p, pe.last(f"out{s}"))
                            d = act(A.activation(full[0:64, NC * s + 2 * half:NC * s + 2 * half + 2, :, 64:128].rearrange("p c h t -> p (c h) t"),
                                                 b[0:64, :].rearrange("p (n t) -> p n t", t=64), ACT.Copy))
                            ring.release(slot, d)
                    read[par] = p
                    offdiag = d
            wait(A, placed)
            wait(V, placed, pe.last("out1"))
            for q in range(4):
                rows = slice(SB * q, SB * q + SB)
                dst = full[rows, :, :, SB * q:SB * q + SB].rearrange("p n h t -> p (n h) t")
                src = diag[rows, :, :, :, :].rearrange("p s c h t -> p (s c h) t")
                if q % 2:
                    filled_a = act(A.activation(dst, src, ACT.Copy), "full")
                else:
                    filled_v = dve(V.tensor_copy(dst, src), "full")
            levels(CH)
            wait(A, summed, dve.last("gp"), dve.last("state"))
            e1 = act(A.activation(gp[:, :], pre[:, :], ACT.Exp, scale=-1.0))
            e2 = act(A.activation(gs[:, :], suf[:, :], ACT.Exp, scale=-1.0), "gp")
            e3 = act(A.activation(decay[:, :], total[CH][:, :], ACT.Exp, scale=-1.0))
            wait(V, e3, pe.last("out1"))
            dve(V.tensor_tensor(qs[:, :], gp[:, :], rec[:, :], ALU.mult), "rec")
            d = dve(V.tensor_tensor(kc[:, :], gs[:, :], key[:, :], ALU.mult), "key")
            k.seen["rw_dve", "gp"] = d[1]
            slot, b = take()
            wait(E, d)
            for n in range(NC):
                p = E.transpose(b[:, n * CH:(n + 1) * CH], kc[:, n * CH:(n + 1) * CH], w("ident"))
            p = pe(p)
            wait(A, p, pe.last("add"))
            t = act(A.activation(kct[:, :], b[:, :], ACT.Copy))
            ring.release(slot, t)
            slot, b = take()
            wait(E, t)
            for s in range(2):
                wait(E, vals[s])
                for n in range(NC):
                    p = E.matmul(b[64 * s:64 * s + KD, n * CH:(n + 1) * CH], kct[:, n * CH + 64 * s:n * CH + 64 * s + KD],
                                 val[s][:, n * CH:(n + 1) * CH], start=True, stop=True)
            p = pe(p, "add")
            wait(V, p)
            masked = dve(V.tensor_tensor(add[:, :, :], b[:, :].rearrange("p (c d) -> p c d", d=CH),
                                         w("statemask").unsqueeze(1).broadcast_to([P, NC, CH]), ALU.mult))
            ring.release(slot, masked)
            wait(V, dve.last("state"))
            st = dve(V.tensor_scalar(state[:, 0, :], carry[:, :], k.w_at("carries", it), None, ALU.mult))
            for n in range(NC):
                wait(V, masked, st)
                dst = state[:, n + 1, :] if n + 1 < NC else carry[:, :]
                st = dve(V.scalar_tensor_tensor(dst, state[:, n, :], decay[:, n:n + 1], add[:, n, :], ALU.mult, ALU.add), "state")
            for s in range(2):
                slot, b = take()
                wait(E, st, filled_a, filled_v, offdiag, vals[s])
                for n in range(NC):
                    cols = slice(n * CH, (n + 1) * CH)
                    E.matmul(b[:, cols], state[64 * s:64 * s + KD, n, :], qs[64 * s:64 * s + KD, cols], start=True, stop=True)
                    for h in range(NH):
                        p = E.matmul(b[DV * h:DV * h + DV, cols], val[s][:, n * CH + DV * h:n * CH + DV * h + DV],
                                     full[:, NC * s + n, h, :], start=False, stop=True, skip_group_check=True)
                p = pe(p, f"out{s}")
                wait(A, p)
                d = act(A.activation(out[:, bass.ds((it + 4 * s) * TILE, TILE)], b[:, :], ACT.Copy))
                ring.release(slot, d)
        stage.over(*k.all_engines())


def recurrence_out(k, w, y, gate, x):
    nc = k.nc
    V, A, E = nc.vector, nc.scalar, nc.tensor
    with ExitStack() as c:
        scaled = [k.sb(f"go_scaled{g}", [P, TILE], ctx=c) for g in range(2)]
        gated = [k.sb(f"go_gated{g}", [P, TILE], ctx=c) for g in range(2)]
        bank = [k.ps(f"go_bank{g}", [P, TILE], c) for g in range(2)]
        stage = Stage(k, "go", NT // 2)
        with stage as (i, pe, dve, act, pool, sp):
            for g in range(2):
                cols = bass.ds((2 * i + g) * TILE, TILE)
                wait(A, dve.last(f"gated{g}"))
                a = act(A.activation(scaled[g][:, :], y[:, cols], ACT.Identity, scale=w("gnw"), bias=w("gnb")))
                wait(V, a, pe.last(f"proj{g}"))
                d = dve(V.scalar_tensor_tensor(gated[g][:, :], scaled[g][:, :], 0.5, gate[:, cols], ALU.mult, ALU.mult), f"gated{g}")
                wait(E, d, dve.last(f"sum{g}"))
                p = pe(E.matmul(bank[g][:, :], w("wo"), gated[g][:, :], start=True, stop=True), f"proj{g}")
            for g in range(2):
                cols = bass.ds((2 * i + g) * TILE, TILE)
                wait(V, (pe, g + 1))
                dve(V.tensor_tensor(x[:, cols], bank[g][:, :], x[:, cols], ALU.add), f"sum{g}")
        stage.over(*k.all_engines())


class Arrivals:

    def __init__(self, k, name, slots, stage):
        self.k, self.name, self.slots, self.stage = k, name, slots, stage
        self.sems = [k.sem(f"{name}{n}") for n in range(len(slots))]
        self.fills = [0] * len(slots)

    def started(self, slot, dma):
        dma.then_inc(self.sems[slot], 16)
        self.fills[slot] += 1
        self.k.seen[self.name, slot, "fills"] = self.fills[slot]
        return slot, self.fills[slot]

    def wait(self, engine, landed):
        slot, n = landed
        per = self.k.counts.get((self.name, slot, "fills"), 1)
        engine.wait_ge(self.sems[slot], self.stage.turn * (16 * per) + 16 * n)


def over(k, arrivals, *engines):
    for e in engines:
        for slot, sem in enumerate(arrivals.sems):
            if arrivals.fills[slot]:
                e.wait_ge(sem, 16 * arrivals.fills[slot] * arrivals.stage.turns)


FH, FE, FI, FD = 8, 16, 64, 16
EP = FE // 2
TERMS = 6
ACT_PARTS = (0, 0, 1, 1, 0, 2)
WEIGHT_PARTS = (0, 1, 0, 1, 2, 0)


def split3(V, lane, src, parts, rest):
    hi, mid, lo = parts
    d = lane(V.tensor_copy(hi, src))
    wait(V, d)
    d = lane(V.tensor_tensor(rest, src, hi, ALU.subtract))
    wait(V, d)
    d = lane(V.tensor_copy(mid, rest))
    wait(V, d)
    return lane(V.tensor_tensor(lo, rest, mid, ALU.subtract))


def top2(k, w, V, A, dve, act, logits, groups, ne, t, weights_of_softmax):
    G3 = [P, groups, ne]
    wide = lambda name: t[name][:, :].unsqueeze(2).broadcast_to(G3)
    order = w("descending", 0, ne).unsqueeze(1).broadcast_to(G3)
    v = lambda name: t[name][:, :].rearrange("p (g e) -> p g e", e=ne)

    def first(src, peak, onehot, ready):
        wait(V, *ready)
        d = dve(V.tensor_reduce(t[peak][:, :], src, AX, ALU.max))
        wait(V, d)
        d = dve(V.tensor_tensor(v("eq"), src, wide(peak), ALU.is_ge))
        wait(V, d)
        d = dve(V.tensor_tensor(v("eq"), v("eq"), order, ALU.mult))
        wait(V, d)
        d = dve(V.tensor_reduce(t["place"][:, :], v("eq"), AX, ALU.max))
        wait(V, d)
        return dve(V.tensor_tensor(v(onehot), order, wide("place"), ALU.is_equal))

    d1 = first(logits, "peak", "one", ())
    wait(V, d1)
    d = dve(V.scalar_tensor_tensor(v("rest"), v("one"), -3e38, logits, ALU.mult, ALU.add))
    off = dve(V.tensor_tensor(v("soft"), logits, wide("peak"), ALU.subtract))
    wait(A, off)
    e = act(A.activation(t["soft"][:, :], t["soft"][:, :], ACT.Exp))
    d2 = first(v("rest"), "peak2", "two", (d,))
    wait(V, d2)
    d = dve(V.tensor_tensor(v("one"), v("one"), v("two"), ALU.add))
    wait(V, d, e)
    chosen = dve(V.tensor_tensor(v("one"), v("one"), v("soft"), ALU.mult))
    if weights_of_softmax:
        d = dve(V.tensor_reduce(t["sum"][:, :], v("soft"), AX, ALU.add))
        wait(V, d)
    else:
        d = dve(V.tensor_reduce(t["sum"][:, :], v("soft"), AX, ALU.add))
        wait(V, chosen)
        d2 = dve(V.tensor_reduce(t["place"][:, :], v("one"), AX, ALU.add))
        wait(V, d, d2)
        d = dve(V.scalar_tensor_tensor(t["sum"][:, :], t["sum"][:, :], 1e-9, t["place"][:, :], ALU.mult, ALU.add))
        wait(V, d)
    d = dve(V.reciprocal(t["sum"][:, :], t["sum"][:, :]))
    wait(V, d, chosen)
    return v, wide, d


def moe0_prepare(k, w, xn, stack, shares):
    nc = k.nc
    V, A, E, S = nc.vector, nc.scalar, nc.tensor, nc.sync
    with ExitStack() as c:
        sb = lambda name, *shape, dt=F32: k.sb(f"mp_{name}", [P, *shape], dt, ctx=c)
        banks = [k.ps(f"mp_bank{n}", [P, TILE], c) for n in range(4)]
        h, rest, sharesT = sb("h", TILE), sb("resth", TILE), sb("sharesT", TILE)
        parts = [sb(f"part{n}", TILE, dt=BF16) for n in range(3)]
        logits = sb("logits", TILE)
        groups = TILE // FE
        t = {n: sb(n, TILE) for n in ("eq", "one", "two", "rest", "soft", "cw")}
        t |= {n: sb(n, groups) for n in ("peak", "peak2", "place", "sum")}
        for name, n in (("mp_parts", TERMS), ("mp_shares", 1)):
            S.sem_inc(k.drain_sem(name, n), 16 * n)
        stage = Stage(k, "mp", NT)
        with stage as (i, pe, dve, act, pool, sp):
            wait(E, act.last("h"))
            p = pe(E.matmul(banks[0][:, :], w("wm"), xn[:, bass.ds(i * PITCH + 1, TILE)], start=True, stop=True))
            wait(A, p, dve.last("split"), pe.last("logits"))
            hd = act(A.activation(h[:, :], banks[0][:, :], ACT.Identity, bias=w("bm")), "h")
            wait(E, hd, act.last("logits"))
            for n in range(NC):
                p = E.matmul(banks[1][:, n * CH:(n + 1) * CH], h[:, n * CH:(n + 1) * CH], w("emb"), start=True, stop=True)
            p = pe(p, "logits")
            wait(A, p, dve.last("topk"))
            lg = act(A.activation(logits[:, :], banks[1][:, :], ACT.Copy), "logits")
            k.drained(V, "mp_parts", i)
            wait(V, hd)
            split3(V, dve, h[:, :], [q[:, :] for q in parts], rest[:, :])
            k.seen["mp_dve", "split"] = dve.pos
            for n in range(TERMS):
                wait(S, (dve, dve.pos))
                dst = stack[bass.ds(i, 1), :, n * FD:(n + 1) * FD, :].rearrange("a h d t -> (a h) d t")
                S.dma_start(dst, parts[ACT_PARTS[n]][:, :]).then_inc(k.drain_sem("mp_parts", TERMS), 16)
            wait(V, lg)
            v, wide, inv = top2(k, w, V, A, dve, act, logits[:, :].rearrange("p (g e) -> p g e", e=FE), groups, FE, t, True)
            wait(V, pe.last("turned"))
            cw = dve(V.tensor_tensor(v("cw"), v("one"), wide("sum"), ALU.mult), "topk")
            wait(E, cw, act.last("shares"))
            for n in range(NC):
                p = E.transpose(banks[2][:, n * CH:(n + 1) * CH], t["cw"][:, n * CH:(n + 1) * CH], w("ident"))
            p = pe(p, "turned")
            k.drained(A, "mp_shares", i)
            wait(A, p)
            a = act(A.activation(sharesT[:, :], banks[2][:, :], ACT.Copy), "shares")
            wait(S, a)
            S.dma_start(shares[bass.ds(i, 1), :, :].rearrange("a q t -> (a q) t"), sharesT[:, :]).then_inc(k.drain_sem("mp_shares", 1), 16)
        stage.over(*k.all_engines())
        for name, n in (("mp_parts", TERMS), ("mp_shares", 1)):
            k.drain_over(name, NT)


def moe0(k, w, stack, shares, x):
    nc = k.nc
    V, A, E, S = nc.vector, nc.scalar, nc.tensor, nc.sync
    with ExitStack() as c:
        sb = lambda name, *shape, dt=F32: k.sb(f"m0_{name}", shape, dt, ctx=c)
        up = [k.ps(f"m0_up{n}", [P, 2, TILE], c) for n in range(2)]
        down = [k.ps(f"m0_down{n}", [P, TILE], c) for n in range(2)]
        comb = k.ps("m0_comb", [P, TILE], c)
        outb = k.ps("m0_out", [P, TILE], c)
        terms = sb("terms", TERMS * FD, 4, TILE, dt=BF16)
        share = sb("share", P, 4, 2, TILE)
        act_h = sb("act_h", P, 2, 4, 2, TILE)
        prod = [sb(f"prod{n}", P, TILE) for n in range(4)]
        combs = [sb(f"combs{n}", P, TILE) for n in range(2)]
        w1s = sb("w1s", TERMS * FD, FE * FI, dt=BF16)
        rows = TERMS * FD
        with ExitStack() as c2:
            w1f = k.sb("m0_w1f", [rows, FE * FI], ctx=c2)
            rest = k.sb("m0_rest", [rows, FE * FI], ctx=c2)
            parts = [k.sb(f"m0_w1p{n}", [rows, FE * FI], BF16, ctx=c2) for n in range(3)]
            got, made = k.sem("m0_w1"), k.sem("m0_split")
            S.dma_start(w1f[:, :], k.dram["w1"]).then_inc(got, 16)
            V.wait_ge(got, 16)
            count = [0]

            def step(ins):
                count[0] += 1
                ins.then_inc(made, 1)
                V.wait_ge(made, count[0])
            step(V.tensor_copy(parts[0][:, :], w1f[:, :]))
            step(V.tensor_tensor(rest[:, :], w1f[:, :], parts[0][:, :], ALU.subtract))
            step(V.tensor_copy(parts[1][:, :], rest[:, :]))
            step(V.tensor_tensor(parts[2][:, :], rest[:, :], parts[1][:, :], ALU.subtract))
            step(V.tensor_scalar(rest[:, :], parts[0][:, :], w("rows0")[0:rows], None, ALU.mult))
            step(V.scalar_tensor_tensor(rest[:, :], parts[1][:, :], w("rows1")[0:rows], rest[:, :], ALU.mult, ALU.add))
            step(V.scalar_tensor_tensor(w1s[:, :], parts[2][:, :], w("rows2")[0:rows], rest[:, :], ALU.mult, ALU.add))
            for e in k.all_engines():
                e.wait_ge(made, count[0])
        stage = Stage(k, "m0", NT)
        with stage as (i, pe, dve, act, pool, sp):
            lanes = stage.lanes
            tarr = Arrivals(k, "m0_tarr", list(range(4)), sp)
            sring = Ring(k, "m0_sring", list(range(4)))
            sarr = Arrivals(k, "m0_sarr", list(range(4)), sp)
            upring = Ring(k, "m0_upring", up)
            dring = Ring(k, "m0_dring", down)
            pring = Ring(k, "m0_pring", prod)
            hring = Ring(k, "m0_hring", list(range(2)))
            cring = Ring(k, "m0_cring", combs)

            def fetch(hd):
                slot = sring.take(S, lanes)
                wait(S)
                src = stack[bass.ds(i, 1), hd, :, :].rearrange("a r t -> (a r) t")
                t = tarr.started(slot, S.dma_start(terms[:, slot, :], src))
                for half in range(2):
                    rows = shares[bass.ds(i, 1), hd * FE + half * 8:hd * FE + half * 8 + 8, :].rearrange("a e t -> (a e) t")
                    src = rows.unsqueeze(1).broadcast_to([8, FD, TILE])
                    s = sarr.started(slot, S.dma_start(share[:, slot, half, :], src))
                return slot, t, s

            got = {hd: fetch(hd) for hd in range(4)}
            units = [(hp, half) for hp in range(4) for half in range(2)]
            act_of = {}
            waited = set()

            def ups(hp, half, e):
                ep = 4 * half + e
                u = upring.take(E, lanes)
                uslot = upring.slot
                for j in range(2):
                    hd = 2 * hp + j
                    if hd not in waited:
                        tarr.wait(E, got[hd][1])
                        waited.add(hd)
                wait(E)
                for j in range(2):
                    slot = got[2 * hp + j][0]
                    p = E.matmul(u[:, j, :], w1s[:, ep * P:(ep + 1) * P], terms[:, slot, :], start=True, stop=True)
                p = pe(p)
                if e == 0:
                    hring.take(A, lanes)
                    act_of[hp, half] = hring.slot
                wait(A, p)
                a = act(A.activation(act_h[:, act_of[hp, half], e, :, :], u[:, :, :], ACT.Gelu, bias=w("b1", ep, ep + 1)))
                upring.release(uslot, a)
                return a

            def downs(hp, half, ready):
                hslot = act_of[hp, half]
                folds = []
                for j in range(2):
                    hd = 2 * hp + j
                    d = dring.take(E, lanes)
                    dslot = dring.slot
                    wait(E, ready)
                    for e in range(4):
                        ep = 4 * half + e
                        p = E.matmul(d[32 * e:32 * e + 32, :], w("w2", 32 * ep, 32 * ep + 32), act_h[:, hslot, e, j, :], start=True, stop=True)
                    p = pe(p)
                    if j == 1:
                        hring.release(hslot, p)
                    pr = pring.take(V, lanes)
                    pslot = pring.slot
                    if half == 0:
                        sarr.wait(V, got[hd][2])
                    wait(V, p)
                    v = dve(V.scalar_tensor_tensor(pr[:, :], d[:, :], w("b2", half, half + 1), share[:, got[hd][0], half, :], ALU.add, ALU.mult))
                    dring.release(dslot, v)
                    if half == 1:
                        sring.release(got[hd][0], v)
                    folds.append((hd, half, pr, pslot, v))
                return folds

            def fold(folds):
                for hd, half, pr, pslot, v in folds:
                    if hd % 4 == 0 and half == 0:
                        wait(E, comb_read[0])
                    wait(E, v)
                    q = hd % 4
                    p = pe(E.matmul(comb[32 * q:32 * q + 32, :], w("fold"), pr[:, :], start=half == 0, stop=half == 1))
                    pring.release(pslot, p)
                    if hd % 4 == 3 and half == 1:
                        cslot_buf = cring.take(A, lanes)
                        cslot = cring.slot
                        wait(A, p)
                        a = act(A.activation(cslot_buf[:, :], comb[:, :], ACT.Copy), "comb")
                        comb_read[0] = a
                        if hd == 3:
                            wait(E, dve.last("sum"))
                        wait(E, a)
                        p = pe(E.matmul(outb[:, :], w(f"wo0{hd // 4}"), cslot_buf[:, :], start=hd == 3, stop=hd == 7))
                        cring.release(cslot, p)
                        if hd == 7:
                            xc = x[:, bass.ds(i * TILE, TILE)]
                            wait(V, p)
                            dve(V.scalar_tensor_tensor(xc, outb[:, :], w("bo"), xc, ALU.add, ALU.add), "sum")

            comb_read = [act.last("comb")]
            later, folding = None, None
            for n, (hp, half) in enumerate(units):
                for e in range(4):
                    a = ups(hp, half, e)
                    if e == 1:
                        if folding:
                            fold(folding)
                            folding = None
                        if later:
                            folding = downs(*later)
                            later = None
                        if half == 0 and 1 <= hp <= 2:
                            for j in range(2):
                                hd = 2 * (hp + 1) + j
                                if hd >= 4:
                                    got[hd] = fetch(hd)
                later = (hp, half, a)
            fold(folding)
            fold(downs(*later))
        stage.over(*k.all_engines())
        over(k, tarr, *k.all_engines())
        over(k, sarr, *k.all_engines())


AH, AD = 16, 8
HG = 4
NG = AH // HG
QB = T // CH
SROWS = 96
MROW = 64
VW = 32
SCALE = AD ** -0.5


def attention_prepare(k, w, xn, qstack, kstack, vstack):
    nc = k.nc
    V, A, E, S = nc.vector, nc.scalar, nc.tensor, nc.sync
    with ExitStack() as c:
        sb = lambda name, *shape, dt=F32: k.sb(f"ap_{name}", [P, *shape], dt, ctx=c)
        banks = [k.ps(f"ap_bank{n}", [P, TILE], c) for n in range(4)]
        latent, rest = sb("latent", TILE), sb("resta", TILE)
        full = {"q": sb("q", TILE), "k": sb("k", TILE)}
        parts = {n: [sb(f"{n}part{m}", TILE, dt=BF16) for m in range(3)] for n in "qk"}
        values = sb("values", NC, VW)
        dmas = {"ap_q": 2 * TERMS, "ap_k": 2 * TERMS, "ap_v": 2}
        for name, n in dmas.items():
            S.sem_inc(k.drain_sem(name, n), 16 * n)
        stage = Stage(k, "ap", NB)
        with stage as (b, pe, dve, act, pool, sp):
            sent = {n: 0 for n in dmas}

            def drained(engine, name):
                engine.wait_ge(k.drain_sem(name, 0), b * (16 * dmas[name]) + 16 * dmas[name] + 16 * sent[name])

            def send(name, dst, src):
                S.dma_start(dst, src).then_inc(k.drain_sem(name, 0), 16)
                sent[name] += 1

            for half in range(2):
                mark = lambda name: act_marks.get(name) or act.last(name)
                act_marks = {} if half == 0 else act_marks
                cols = bass.ds((2 * b + half) * TILE, TILE)
                wait(E, mark("latent"))
                p = pe(E.matmul(banks[0][:, :], w("wdown"), xn[:, cols], start=True, stop=True))
                wait(A, p, pe.last("values") if half == 0 else values_read)
                lat = act_marks["latent"] = act(A.activation(latent[:, :], banks[0][:, :], ACT.Copy), "latent")
                for n, (name, rows, bank) in enumerate((("q", P, banks[1]), ("k", 32, banks[2]))):
                    wait(E, lat, mark(name))
                    p = pe(E.matmul(bank[0:rows, :], w(f"w{name}up"), latent[:, :], start=True, stop=True))
                    wait(A, p, dve.last(f"split{name}") if half == 0 else split[name])
                    a = act_marks[name] = act(A.activation(full[name][0:rows, :], bank[0:rows, :], ACT.Copy), name)
                    drained(V, f"ap_{name}")
                    wait(V, a)
                    d = split3(V, dve, full[name][0:rows, :], [q[0:rows, :] for q in parts[name]], rest[0:rows, :])
                    k.seen["ap_dve", f"split{name}"] = d[1]
                    split = {} if n == 0 and half == 0 else split
                    split[name] = d
                    wait(S, d)
                    src = (ACT_PARTS, WEIGHT_PARTS)[n]
                    for m in range(TERMS):
                        rows_ = slice(m * AD, (m + 1) * AD)
                        if name == "q":
                            dst = qstack[bass.ds(b, 1), :, rows_, half * TILE:(half + 1) * TILE].rearrange("a h d t -> (a h) d t")
                            send("ap_q", dst, parts["q"][src[m]][:, :])
                        else:
                            dst = kstack[bass.ds(b, 1), :, rows_, half * TILE:(half + 1) * TILE].rearrange("a g d t -> d (a g) t")
                            send("ap_k", dst, parts["k"][src[m]][0:AD, :].unsqueeze(1).broadcast_to([AD, NG, TILE]))
                wait(E, dve.last("values") if half == 0 else valued)
                for n in range(NC):
                    p = E.matmul(banks[3][:, n * VW:(n + 1) * VW], latent[:, n * CH:(n + 1) * CH], w("wvup"), start=True, stop=True)
                values_read = p = pe(p, "values")
                drained(V, "ap_v")
                wait(V, p)
                valued = dve(V.tensor_tensor(values[:, :, :], banks[3][:, 0:NC * VW].rearrange("p (n v) -> p n v", v=VW),
                                             w("sumcolumn").unsqueeze(1).broadcast_to([P, NC, VW]), ALU.add), "values")
                wait(S, valued)
                dst = vstack[bass.ds(b, 1), :, :, half * NC * VW:(half + 1) * NC * VW].rearrange("a g p v -> p (a g) v")
                send("ap_v", dst, values[:, :, :].rearrange("p n v -> p (n v)").unsqueeze(1).broadcast_to([P, NG, NC * VW]))
        stage.over(*k.all_engines())
        for name in dmas:
            k.drain_over(name, NB)


def attention_max(k, w, qstack, kstack, maxima):
    nc = k.nc
    V, A, E, S = nc.vector, nc.scalar, nc.tensor, nc.sync
    with ExitStack() as c:
        sb = lambda name, *shape, dt=F32: k.sb(f"am_{name}", [P, *shape], dt, ctx=c)
        score = [k.ps(f"am_score{n}", [P, 2, TILE], c) for n in range(3)]
        turned = k.ps("am_turned", [HG * QB, CH], c)
        qs, ks = sb("qs", 2, HG, T, dt=BF16), sb("ks", 2, T, dt=BF16)
        peaks, top, rest = sb("peaks", HG, QB, 2), sb("top", HG * QB), sb("restm", CH)
        rows = sb("rows", CH)
        parts = [sb(f"part{n}", CH, dt=BF16) for n in range(3)]
        zero = k.sem("am_zero")
        V.memset(qs[:, :, :, :], 0.0).then_inc(zero, 1)
        V.memset(ks[:, :, :], 0.0).then_inc(zero, 1)
        V.memset(peaks[:, :, :, :], -3e38).then_inc(zero, 1)
        for e in k.all_engines():
            e.wait_ge(zero, 3)
        S.sem_inc(k.drain_sem("am_max", 3 * 2), 16 * 6)
        stage = Stage(k, "am", NB * NG // 2)
        with stage as (i, pe, dve, act, pool, sp):
            lanes = stage.lanes
            ring = Ring(k, "am_ring", score)
            qring, qarr = Ring(k, "am_qring", [0, 1]), Arrivals(k, "am_qarr", [0, 1], sp)
            karr = Arrivals(k, "am_karr", [0, 1], sp)
            fetched = []
            for u in range(2):
                slot = qring.take(S, lanes)
                wait(S)
                src = qstack.rearrange("b (g a) r t -> (b g) r a t", a=HG)[bass.ds(2 * i + u, 1)].rearrange("x r a t -> (x r) a t")
                q = qarr.started(slot, S.dma_start(qs[0:TERMS * AD, slot, :, :], src))
                src = kstack.rearrange("b g r t -> (b g) r t")[bass.ds(2 * i + u, 1)].rearrange("x r t -> (x r) t")
                kk = karr.started(slot, S.dma_start(ks[0:TERMS * AD, slot, :], src))
                fetched.append((slot, q, kk))
            for u in range(2):
                slot, q, kk = fetched[u]
                qarr.wait(E, q)
                karr.wait(E, kk)
                reduced = None
                for blk in range(QB):
                    for seg in range(blk // 4 + 1):
                        n = min(TILE, (blk + 1) * CH - seg * TILE)
                        for hp in range(2):
                            t = ring.take(E, lanes)
                            rslot = ring.slot
                            wait(E)
                            for j in range(2):
                                p = E.matmul(t[:, j, 0:n], qs[0:SROWS, slot, 2 * hp + j, blk * CH:(blk + 1) * CH],
                                             ks[0:SROWS, slot, seg * TILE:seg * TILE + n], start=True, stop=True)
                                if seg == blk // 4:
                                    p = E.matmul(t[:, j, n - CH:n], k.bf["ident"], k.bf["later_s"],
                                                 start=False, stop=True, skip_group_check=True)
                            p = pe(p)
                            wait(V, p, dve.last("top") if u == 0 else topped)
                            reduced = dve(V.tensor_reduce(peaks[:, 2 * hp:2 * hp + 2, blk, seg], t[:, :, 0:n], AX, ALU.max))
                            ring.release(rslot, reduced)
                qring.release(slot, p)
                wait(V, reduced, pe.last("turn") if u == 0 else turned_by)
                topped = dve(V.tensor_reduce(top[:, :], peaks[:, :, :, :].rearrange("p a q s -> p (a q) s"), AX, ALU.max, negate=True), "top")
                wait(E, topped, dve.last("rows") if u == 0 else rowed)
                turned_by = pe(E.transpose(turned[:, :], top[:, :], w("ident")), "turn")
                wait(V, turned_by)
                nr = HG * QB
                V.wait_ge(k.drain_sem("am_max", 0), i * (16 * 6) + 16 * (6 + 3 * u))
                rowed = dve(V.tensor_copy(rows[0:nr, :], turned[:, :]), "rows")
                wait(V, rowed)
                d = split3(V, dve, rows[0:nr, :], [q_[0:nr, :] for q_ in parts], rest[0:nr, :])
                wait(S, d)
                for m in range(3):
                    dst = maxima[bass.ds(2 * i + u, 1), m, :].rearrange("x (q t) -> (x q) t", t=CH)
                    S.dma_start(dst, parts[m][0:nr, :]).then_inc(k.drain_sem("am_max", 0), 16)
        stage.over(*k.all_engines())
        over(k, qarr, *k.all_engines())
        over(k, karr, *k.all_engines())
        k.drain_over("am_max", NB * NG // 2)


def attention_sum(k, w, qstack, kstack, vstack, maxima, y):
    nc = k.nc
    V, A, E, S = nc.vector, nc.scalar, nc.tensor, nc.sync
    with ExitStack() as c:
        sb = lambda name, *shape, dt=F32: k.sb(f"ax_{name}", [P, *shape], dt, ctx=c)
        score = [k.ps(f"ax_score{n}", [P, 2, TILE], c) for n in range(3)]
        sums = [k.ps(f"ax_sums{n}", [P, TILE], c) for n in range(2)]
        qs, ks = sb("qs", 2, HG, T, dt=BF16), sb("ks", 2, T, dt=BF16)
        vs = sb("vs", 2, QB, VW)
        prob = sb("prob", 2, HG, TILE)
        zero = k.sem("ax_zero")
        V.memset(qs[:, :, :, :], 0.0).then_inc(zero, 1)
        V.memset(ks[:, :, :], 0.0).then_inc(zero, 1)
        V.wait_ge(zero, 2)
        V.memset(ks[MROW:MROW + 3, :, :], 1.0).then_inc(zero, 1)
        for e in k.all_engines():
            e.wait_ge(zero, 3)
        stage = Stage(k, "ax", NB * NG // 2)
        with stage as (i, pe, dve, act, pool, sp):
            lanes = stage.lanes
            ring, sring, pring = Ring(k, "ax_ring", score), Ring(k, "ax_sring", sums), Ring(k, "ax_pring", [0, 1])
            qring = Ring(k, "ax_qring", [0, 1])
            arr = [Arrivals(k, f"ax_{n}arr", [0, 1], sp) for n in "qkvm"]
            fetched = []
            for u in range(2):
                slot = qring.take(S, lanes)
                wait(S)
                turn = bass.ds(2 * i + u, 1)
                src = [qstack.rearrange("b (g a) r t -> (b g) r a t", a=HG)[turn].rearrange("x r a t -> (x r) a t"),
                       kstack.rearrange("b g r t -> (b g) r t")[turn].rearrange("x r t -> (x r) t"),
                       vstack.rearrange("b g p v -> (b g) p v")[turn].rearrange("x p v -> (x p) v"),
                       maxima[turn].rearrange("x m t -> (x m) t")]
                dst = [qs[0:TERMS * AD, slot, :, :], ks[0:TERMS * AD, slot, :], vs[:, slot, :, :].rearrange("p q v -> p (q v)"),
                       qs[MROW:MROW + 3, slot, :, :].rearrange("p a t -> p (a t)")]
                fetched.append((slot, [a.started(slot, S.dma_start(d_, s_)) for a, d_, s_ in zip(arr, dst, src)]))
            later = []

            def weigh(task):
                slot, blk, off, pslot, a, th, bank, bslot, nblk = task
                if blk == 0:
                    sring_marks = sring_take(th, bslot)
                wait(E, a)
                for h in range(HG):
                    p = E.matmul(bank[VW * h:VW * h + VW, off:TILE], vs[:, slot, blk, :], prob[:, pslot, h, off:TILE],
                                 start=blk == 0, stop=True, skip_group_check=True)
                p = pe(p)
                pring.release(pslot, p)
                if blk == nblk - 1:
                    wait(V, p)
                    u = fetched.index(next(f for f in fetched if f[0] == slot))
                    d = dve(V.tensor_copy(y[:, bass.ds((2 * i + u) * T + th * TILE, TILE)], bank[:, :]))
                    sring.release(bslot, d)
                return p

            def sring_take(th, bslot):
                pass

            for u in range(2):
                slot, landed = fetched[u]
                for a_, l in zip(arr, landed):
                    a_.wait(E, l)
                for th in range(2):
                    bank = bslot = None
                    nblk = 4 * (th + 1)
                    for blk in range(nblk):
                        off = max(0, blk * CH - th * TILE)
                        pslot = None
                        for hp in range(2):
                            t = ring.take(E, lanes)
                            rslot = ring.slot
                            wait(E)
                            for j in range(2):
                                h = 2 * hp + j
                                p = E.matmul(t[:, j, off:TILE], ks[0:SROWS, slot, blk * CH:(blk + 1) * CH],
                                             qs[0:SROWS, slot, h, th * TILE + off:(th + 1) * TILE], start=True, stop=True)
                                if blk >= 4 * th:
                                    p = E.matmul(t[:, j, off:off + CH], k.bf["ident"], k.bf["earlier_t"],
                                                 start=False, stop=True, skip_group_check=True)
                            p = pe(p)
                            if hp == 0:
                                pslot = pring.take(A, lanes)
                            wait(A, p)
                            a = act(A.activation(prob[:, pslot, 2 * hp:2 * hp + 2, off:TILE], t[:, :, off:TILE], ACT.Exp, scale=SCALE))
                            ring.release(rslot, a)
                            if hp == 0 and later:
                                last = weigh(later.pop())
                        if blk == 0:
                            bank = sring.take(E, lanes)
                            bslot = sring.slot
                        later.append((slot, blk, off, pslot, a, th, bank, bslot, nblk))
                last = weigh(later.pop())
                qring.release(slot, last)
        stage.over(*k.all_engines())
        for a in arr:
            over(k, a, *k.all_engines())


def attention_out(k, w, y, x):
    nc = k.nc
    V, A, E, S = nc.vector, nc.scalar, nc.tensor, nc.sync
    cols = NB * NG * T
    sums = nc.dram_tensor("sums", (HG, cols), F32, kind="Internal").ap()
    inverse = nc.dram_tensor("inverse", (HG, cols), F32, kind="Internal").ap()
    with ExitStack() as c:
        dense = k.sb("ao_dense", [P, HG * cols // P], ctx=c)
        inv = k.sb("ao_inv", [P, 2, NG, T], ctx=c)
        bank = [k.ps(f"ao_bank{n}", [P, TILE], c) for n in range(4)]
        moved, inverted = k.sem("ao_moved"), k.sem("ao_inverted")
        for h in range(HG):
            S.dma_start(sums[h:h + 1, :], y[VW * h + AD:VW * h + AD + 1, :]).then_inc(moved, 16)
        S.wait_ge(moved, 16 * HG)
        flat = lambda t: t.rearrange("h (p n) -> (h p) n", p=P // HG)
        S.dma_start(dense[:, :], flat(sums)).then_inc(moved, 16)
        V.wait_ge(moved, 16 * (HG + 1))
        V.reciprocal(dense[:, :], dense[:, :]).then_inc(inverted, 1)
        S.wait_ge(inverted, 1)
        S.dma_start(flat(inverse), dense[:, :]).then_inc(moved, 16)
        S.wait_ge(moved, 16 * (HG + 2))
        stage = Stage(k, "ao", NB // 2)
        with stage as (i, pe, dve, act, pool, sp):
            lanes = stage.lanes
            ring = Ring(k, "ao_ring", bank)
            iring, iarr = Ring(k, "ao_iring", [0, 1]), Arrivals(k, "ao_iarr", [0, 1], sp)
            got = []
            for u in range(2):
                slot = iring.take(S, lanes)
                wait(S)
                src = inverse[:, bass.ds((2 * i + u) * NG * T, NG * T)].unsqueeze(1).broadcast_to([HG, VW, NG * T])
                got.append((slot, iarr.started(slot, S.dma_start(inv[:, slot, :, :].rearrange("p g t -> p (g t)"), src))))
            for u in range(2):
                slot, landed = got[u]
                iarr.wait(V, landed)
                yb = [y[:, bass.ds(((2 * i + u) * NG + g) * T, T)] for g in range(NG)]
                d = []
                for g in range(NG):
                    wait(V)
                    d.append(dve(V.tensor_tensor(inv[:, slot, g, :], inv[:, slot, g, :], yb[g], ALU.mult)))
                for half in range(2):
                    t = ring.take(E, lanes)
                    rslot = ring.slot
                    for g in range(NG):
                        wait(E, d[g])
                        p = E.matmul(t[:, :], w(f"wproj{g}"), inv[:, slot, g, half * TILE:(half + 1) * TILE], start=g == 0, stop=g == NG - 1)
                    p = pe(p)
                    xc = x[:, bass.ds((2 * (2 * i + u) + half) * TILE, TILE)]
                    wait(V, p)
                    v = dve(V.tensor_tensor(xc, t[:, :], xc, ALU.add))
                    ring.release(rslot, v)
                iring.release(slot, p)
        stage.over(*k.all_engines())
        over(k, iarr, *k.all_engines())


ME, MF = 8, 256


def moe1(k, w, z, zn, eps, loops):
    nc = k.nc
    V, A, E, S = nc.vector, nc.scalar, nc.tensor, nc.sync
    with ExitStack() as c:
        sb = lambda name, *shape, dt=F32: k.sb(f"m1_{name}", [P, *shape], dt, ctx=c)
        w13 = sb("w13", ME, 2, MF)
        w2 = sb("w2", ME, 2, HID)
        landed = k.sem("m1_landed")
        S.dma_start(w13[:, :, :, :].rearrange("p e a f -> p (e a f)"), k.dram["w13"]).then_inc(landed, 16)
        S.dma_start(w2[:, :, :, :].rearrange("p e a f -> p (e a f)"), k.dram["w2b"]).then_inc(landed, 16)
        E.wait_ge(landed, 32)
        nt = N // CH
        share = sb("share", nt * ME)
        for loop in range(loops):
            tag = f"m1{loop}"
            normalise(k, f"{tag}n", lambda t: z[:, bass.ds(t * TILE, TILE)], lambda t: zn[:, bass.ds(t * TILE, TILE)],
                      w("mean128"), eps, 4, centre=False, gain=w("normw"))
            with ExitStack() as c2:
                bank = k.ps(f"{tag}_router", [P, nt * ME], c2)
                t = {n: k.sb(f"{tag}_{n}", [P, nt * ME], ctx=c2) for n in ("eq", "one", "two", "rest", "soft", "logits")}
                t |= {n: k.sb(f"{tag}_{n}", [P, nt], ctx=c2) for n in ("peak", "peak2", "place", "sum")}
                lane = {n: Lane(k, e, f"{tag}r_{n}", 0, 1) for n, e in (("dve", V), ("act", A), ("pe", E))}
                for l in lane.values():
                    l.engine.sem_inc(l.sem, l.per)
                for n in range(nt):
                    p = E.matmul(bank[:, n * ME:(n + 1) * ME], zn[:, n * CH:(n + 1) * CH], w("router"), start=True, stop=True)
                p = lane["pe"](p)
                wait(A, p)
                a = lane["act"](A.activation(t["logits"][:, :], bank[:, :], ACT.Copy))
                wait(V, a)
                v, wide, inv = top2(k, w, V, A, lane["dve"], lane["act"], t["logits"][:, :].rearrange("p (g e) -> p g e", e=ME), nt, ME, t, False)
                d = lane["dve"](V.tensor_tensor(share[:, :].rearrange("p (g e) -> p g e", e=ME), v("one"), wide("sum"), ALU.mult))
                for l in lane.values():
                    k.seen[l.name] = l.pos
                for e in k.all_engines():
                    wait(e, d)
            with ExitStack() as c2:
                s2 = lambda name, *shape: k.sb(f"{tag}_{name}", [P, *shape], ctx=c2)
                up = [k.ps(f"{tag}_up{n}", [P, TILE], c2) for n in range(5)]
                down = [k.ps(f"{tag}_down{n}", [P, NC, HID], c2) for n in range(2)]
                back = k.ps(f"{tag}_back", [P, TILE], c2)
                silu = [s2(f"silu{n}", TILE) for n in range(3)]
                hid = [s2(f"hid{n}", TILE) for n in range(4)]
                mixed = [s2(f"mixed{n}", HID) for n in range(NC)]
                stage = Stage(k, tag, NT)
                with stage as (i, pe, dve, act, pool, sp):
                    lanes = stage.lanes
                    upring, dring = Ring(k, f"{tag}_upr", up), Ring(k, f"{tag}_dr", down)
                    sring, hring = Ring(k, f"{tag}_sr", silu), Ring(k, f"{tag}_hr", hid)
                    zt = zn[:, bass.ds(i * TILE, TILE)]
                    added = [None] * NC

                    def ups(e, f):
                        ab = []
                        for a_ in range(2):
                            t_ = upring.take(E, lanes)
                            uslot = upring.slot
                            wait(E)
                            ab.append((t_, uslot, pe(E.matmul(t_[:, :], w13[:, e, a_, f * P:(f + 1) * P], zt, start=True, stop=True))))
                        (ta, sa, pa), (tb, sb_, pb) = ab
                        s_ = sring.take(A, lanes)
                        sslot = sring.slot
                        wait(A, pa)
                        a_ = act(A.activation(s_[:, :], ta[:, :], ACT.Silu))
                        upring.release(sa, a_)
                        h_ = hring.take(V, lanes)
                        hslot = hring.slot
                        wait(V, a_, pb)
                        d_ = dve(V.tensor_tensor(h_[:, :], s_[:, :], tb[:, :], ALU.mult))
                        upring.release(sb_, d_)
                        sring.release(sslot, d_)
                        return h_, hslot, d_

                    def downs(e, hs):
                        t_ = dring.take(E, lanes)
                        dslot = dring.slot
                        wait(E, *[h_[2] for h_ in hs])
                        for n in range(NC):
                            for f in range(2):
                                p_ = E.matmul(t_[:, n, :], hs[f][0][:, n * CH:(n + 1) * CH], w2[:, e, f, :], start=f == 0, stop=f == 1)
                        p_ = pe(p_)
                        for h_ in hs:
                            hring.release(h_[1], p_)
                        wait(V, p_)
                        for n in range(NC):
                            g = share[:, bass.ds((i * NC + n) * ME + e, 1)]
                            if e == 0:
                                wait(V, pe.last("turn"))
                                d_ = added[n] = dve(V.tensor_scalar(mixed[n][:, :], t_[:, n, :], g, None, ALU.mult))
                            else:
                                wait(V, added[n])
                                d_ = added[n] = dve(V.scalar_tensor_tensor(mixed[n][:, :], t_[:, n, :], g, mixed[n][:, :], ALU.mult, ALU.add))
                        dring.release(dslot, d_)

                    later = None
                    for e in range(ME):
                        hs = [ups(e, 0)]
                        if later:
                            downs(*later)
                        hs.append(ups(e, 1))
                        later = (e, hs)
                    downs(*later)
                    wait(E, *added, dve.last("z"))
                    for n in range(NC):
                        p = E.transpose(back[:, n * CH:(n + 1) * CH], mixed[n][:, :], w("ident"))
                    p = pe(p, "turn")
                    zc = z[:, bass.ds(i * TILE, TILE)]
                    wait(V, p)
                    dve(V.tensor_tensor(zc, back[:, :], zc, ALU.add), "z")
                stage.over(*k.all_engines())


def program(nc, dram, counts, upto=99):
    with ExitStack() as ctx:
        k = Kit(nc, ctx, counts, dram)
        x = k.sb("x", [P, N])
        const = k.sb("const", list(dram["const"].shape))
        landed = k.sem("landed")

        def w(name, a=0, b=None):
            off, width = COLS[name]
            return const[:, off + a:off + (width if b is None else b)]

        k.w_at = lambda name, i: const[:, bass.ds(COLS[name][0] + i, 1)]
        n = load(k, landed, 0, (x[:, :], dram["x"]), (const[:, :], dram["const"]))
        zero = k.sem("zero")
        eps = k.sb("eps", [P, 1])
        nc.vector.memset(eps[:, :], 1e-5).then_inc(zero, 1)
        k.bf = {}
        nc.vector.wait_ge(landed, n)
        for name in ("ident", "later_s", "earlier_t"):
            t = k.sb(f"bf_{name}", [P, P], BF16)
            nc.vector.tensor_copy(t[:, :], w(name)).then_inc(zero, 1)
            k.bf[name] = t[:, :]
        with ExitStack() as c0:
            xn = k.sb("xn", [P, (NT + 1) * PITCH], ctx=c0)
            nc.vector.memset(xn[:, 0:1], 0.0).then_inc(zero, 1)
            for e in k.all_engines():
                e.wait_ge(landed, n)
                e.wait_ge(zero, 5)

            def last_token(t, dve, out):
                wait(nc.vector, out)
                dve(nc.vector.tensor_scalar(xn[:, bass.ds((t + 1) * PITCH, 1)], xn[:, bass.ds(t * PITCH + TILE, 1)], k.w_at("follows", t), None, ALU.mult))

            normalise(k, "ln0", lambda t: x[:, bass.ds(t * TILE, TILE)], lambda t: xn[:, bass.ds(t * PITCH + 1, TILE)],
                      w("mean128"), eps, 4, extra=last_token)
            if 1 < upto and upto != 50:
                with ExitStack() as c1:
                    out = k.sb("rw_out", [P, N], ctx=c1)
                    gate = k.sb("rw_gate", [P, N], ctx=c1)
                    recurrence(k, w, xn, out, gate)
                    normalise(k, "gn", lambda t: out[:, bass.ds(t * TILE, TILE)], lambda t: out[:, bass.ds(t * TILE, TILE)],
                              w("mean32"), eps, 4)
                    recurrence_out(k, w, out, gate, x)
            if upto > 2:
                stack = nc.dram_tensor("stack", (NT, FH, TERMS * FD, TILE), BF16, kind="Internal").ap()
                shares = nc.dram_tensor("shares", (NT, FH * FE, TILE), F32, kind="Internal").ap()
                moe0_prepare(k, w, xn, stack, shares)
        if upto > 2:
            moe0(k, w, stack, shares, x)
        if upto > 3:
            z, zn = k.sb("z", [P, N]), k.sb("zn", [P, N])
            tile = lambda buf: lambda t: buf[:, bass.ds(t * TILE, TILE)]
            normalise(k, "ln1", tile(x), tile(z), w("mean128"), eps, 4)
            if upto != 61:
                attention(k, w, z, x)
            if upto != 62:
                nc.vector.memset(eps[:, :], 1e-6).then_inc(zero, 1)
                for e in k.all_engines():
                    e.wait_ge(zero, 6)
                moe1(k, w, z, zn, eps, 2)
                wait_all = k.sem("final")
                nc.vector.tensor_tensor(x[:, :], x[:, :], z[:, :], ALU.add).then_inc(wait_all, 1)
                nc.sync.wait_ge(wait_all, 1)
        stored = k.sem("stored")
        nc.sync.dma_start(dram["out"], x[:, :]).then_inc(stored, 16)
        nc.sync.wait_ge(stored, 16)
        return k.seen


def attention(k, w, xn, x):
    nc = k.nc
    scratch = lambda name, shape, dt: nc.dram_tensor(name, shape, dt, kind="Internal").ap()
    qstack = scratch("qstack", (NB, AH, TERMS * AD, T), BF16)
    kstack = scratch("kstack", (NB, NG, TERMS * AD, T), BF16)
    vstack = scratch("vstack", (NB, NG, P, QB * VW), F32)
    maxima = scratch("maxima", (NB * NG, 3, HG * T), BF16)
    with ExitStack() as c:
        attention_prepare(k, w, xn, qstack, kstack, vstack)
        attention_max(k, w, qstack, kstack, maxima)
        y = k.sb("y", [P, NB * NG * T], ctx=c)
        attention_sum(k, w, qstack, kstack, vstack, maxima, y)
        attention_out(k, w, y, x)


COLS = {}


def pack(parts):
    import numpy as np
    off, out = 0, []
    for name, a in parts:
        a = np.asarray(a)
        if a.shape[0] < P:
            a = np.concatenate([a, np.zeros((P - a.shape[0], a.shape[1]), a.dtype)])
        COLS[name] = (off, a.shape[1])
        off += a.shape[1]
        out.append(a)
    return np.ascontiguousarray(np.concatenate(out, axis=1))


def arrays(**inputs):
    import numpy as np
    g = {n: np.asarray(a) for n, a in inputs.items()}
    a = {n[8:]: v for n, v in g.items() if n.startswith("L0_attn_")}
    f32 = np.float32
    col = lambda v: v.reshape(-1, 1)
    pad = lambda m, cols: np.concatenate([m, np.zeros((m.shape[0], cols - m.shape[1]), m.dtype)], axis=1)
    part = np.arange(P)
    x0t = a["W_x0"].T
    x2 = a["W_x2"].reshape(HID, 5, 32)
    parts = [("mean128", np.full((P, P), 1 / P, f32)),
             ("mean32", np.kron(np.eye(4, dtype=f32), np.full((32, 32), 1 / 32, f32))),
             ("ident", np.eye(P, dtype=f32)),
             ("follows", np.tile(np.array([1, 0], f32), (P, NT // 2))),
             ("carries", np.tile(np.array([0, 1], f32), (P, NT // 4))),
             ("headmask", ((part[:, None] % KD) // DK == np.arange(NH)).astype(f32)),
             ("statemask", ((part[:, None] % KD) // DK == part // DV).astype(f32)),
             ("eye32", (part[:, None] % SB == np.arange(SB)).astype(f32))]
    s32 = part[:, None] % SB
    for h in LOW:
        right = np.array([t for t in range(SB) if (t // h) % 2])
        parts.append((f"mask{h}", ((s32 // (2 * h) == right // (2 * h)) & ((s32 // h) % 2 == 0)).astype(f32)))
    parts += [("mu0", col(a["mu0"])), ("wx00", x0t[:, :P]), ("wx01", pad(x0t[:, P:], P)), ("xbias", a["x_bias"].T)]
    for i in range(5):
        m = np.zeros((P, P), f32)
        m[32 * (i % 4):32 * (i % 4) + 32] = x2[:, i, :].T
        parts.append((f"wx2{i}", m))
    parts += [("wr", a["W_r"].T), ("wk", a["W_k"].T), ("ww1", pad(a["W_w1"].T, P)), ("ww2", a["W_w2"].T),
              ("bw2", np.tile(col(a["b_w2"]), (2, 1))), ("bonus", np.tile(col(a["bonus"].reshape(-1)), (2, 1))),
              ("wv", a["W_v"].T), ("wg", a["W_g"].T), ("wo", a["W_o"].T), ("gnw", col(a["gn_weight"])), ("gnb", col(a["gn_bias"]))]
    g0 = {n[7:]: v for n, v in g.items() if n.startswith("L0_ffn_")}
    emb = np.zeros((P, P), f32)
    for n in range(FH):
        emb[n * FD:(n + 1) * FD, n * FE:(n + 1) * FE] = g0["expert_emb"]
    wo0 = g0["Wo"].reshape(2, 4, FD, HID)
    parts += [("wm", g0["Wm"]), ("bm", col(g0["bm"])), ("emb", emb),
              ("descending", np.tile(np.arange(16, 0, -1).astype(f32), (P, 1))),
              ("fold", np.concatenate([(part[:, None] % FD == np.arange(FD)).astype(f32), np.zeros((P, FD), f32)], axis=1)),
              ("b1", g0["b1"].reshape(EP, P).T), ("b2", g0["b2"].reshape(2, P).T), ("bo", col(g0["bo"]))]
    for n in range(3):
        parts.append((f"rows{n}", col(np.repeat(np.array([p == n for p in WEIGHT_PARTS], f32), FD))))
    for n in range(2):
        m = np.zeros((4, 2 * FD, HID), f32)
        m[:, :FD] = wo0[n]
        parts.append((f"wo0{n}", m.reshape(P, HID)))
    w2 = np.zeros((EP, 2, FI, 2, FD), f32)
    for n in range(2):
        w2[:, n, :, n, :] = g0["W2"].reshape(EP, 2, FI, FD)[:, n]
    parts.append(("w2", np.transpose(w2.reshape(EP, P, 2 * FD), (1, 0, 2)).reshape(P, EP * 2 * FD)))
    w1 = np.ascontiguousarray(np.tile(np.transpose(g0["W1"], (1, 0, 2)).reshape(FD, FE * FI), (TERMS, 1)))
    a1 = {n[8:]: v for n, v in g.items() if n.startswith("L1_attn_")}
    f1 = {n[7:]: v for n, v in g.items() if n.startswith("L1_ffn_")}
    later = np.where(part[None, :] > part[:, None], f32(-1e30), f32(0))
    proj = a1["Wc_proj"].reshape(NG, HG, AD, HID)
    parts += [("wdown", pad(a1["Wc_down"], P)), ("wqup", a1["Wq_up"]), ("wkup", pad(a1["Wkv_up"][:, :AD], 32)),
              ("wvup", pad(a1["Wkv_up"][:, AD:], VW)), ("later_s", later), ("earlier_t", later.T),
              ("sumcolumn", np.tile((np.arange(VW) == AD).astype(f32), (P, 1))),
              ("normw", col(f1["norm_w"])), ("router", f1["router_w"])]
    for n in range(NG):
        m = np.zeros((HG, VW, HID), f32)
        m[:, :AD] = proj[n]
        parts.append((f"wproj{n}", m.reshape(P, HID)))
    w13 = np.transpose(np.stack([f1["w1"], f1["w3"]], axis=1), (2, 0, 1, 3)).reshape(HID, -1)
    w2b = np.transpose(f1["w2"].reshape(ME, 2, P, HID), (2, 0, 1, 3)).reshape(P, -1)
    return {"w13": np.ascontiguousarray(w13), "w2b": np.ascontiguousarray(w2b), "w1": w1, "x": np.ascontiguousarray(a["hidden_states"].reshape(N, HID).T), "const": pack(parts)}


def make(bacc, ins, upto=99):
    counts = {}
    for _ in range(2):
        nc = bacc("TRN2", target_bir_lowering=False, num_devices=1)
        dram = {n: nc.dram_tensor(f"in_{n}", v.shape, mybir.dt.from_np(v.dtype), kind="ExternalInput").ap() for n, v in ins.items()}
        dram["out"] = nc.dram_tensor("out_0", (P, N), F32, kind="ExternalOutput").ap()
        counts = program(nc, dram, counts, upto)
    return nc


def kernel(**inputs):
    import concourse.bacc as bacc
    import numpy as np
    from concourse.bass_utils import run_bass_kernel_spmd

    ins = arrays(**inputs)
    nc = make(bacc.Bacc, ins)
    r = run_bass_kernel_spmd(nc, [{f"in_{n}": a for n, a in ins.items()}], core_ids=[0])
    return np.ascontiguousarray(r.results[0]["out_0"].T).reshape(NB, T, HID)
```

```python
from contextlib import ExitStack

import concourse.bass as bass
from concourse import mybir

F32 = mybir.dt.float32
BF16 = mybir.dt.bfloat16
U32 = mybir.dt.uint32
ALU = mybir.AluOpType
ACT = mybir.ActivationFunctionType
AX = mybir.AxisListType.X


class Lane:

    def __init__(self, k, engine, name, turn, turns):
        self.k, self.engine, self.turn, self.turns, self.pos = k, engine, turn, turns, 0
        self.name = name
        self.key = name.rsplit("_", 1)[1]
        self.sem = k.sem(name)
        self.per = k.counts.get(name, 1)
        self.waited = {}

    def __call__(self, instruction, name=None):
        instruction.then_inc(self.sem, 1)
        self.pos += 1
        if name:
            self.k.seen[self.name, name] = self.pos
        return (self, self.pos)

    def last(self, name):
        return (self, self.k.counts.get((self.name, name), 1) - self.per)


def wait(engine, *marks):
    latest = {}
    for lane, pos in (*marks, *owed.pop(id(engine), ())):
        latest[lane] = max(pos, latest.get(lane, pos))
    due = []
    for lane, pos in latest.items():
        if pos > lane.waited.get(id(engine), -lane.per):
            lane.waited[id(engine)] = pos
            due.append((lane.sem, lane.turn * lane.per + (lane.per + pos)))
    for sem, value in due:
        engine.wait_ge(sem, value)


owed = {}


class Task:

    def __init__(self, k, name):
        self.k, self.name = k, name
        nc = k.nc
        self.engines = {"pe": nc.tensor, "dve": nc.vector, "act": nc.scalar, "pool": nc.gpsimd, "sp": nc.sync}
        self.lanes = {e: Lane(k, eng, f"{name}_{e}", 0, 0) for e, eng in self.engines.items()}
        self.ends = []

    def body(self, steps):
        self.steps = steps


def finish(steps):
    while True:
        try:
            next(steps)
        except StopIteration as stop:
            return stop.value


def run(k, turns, *tasks):
    nc = k.nc
    for t in tasks:
        for lane in t.lanes.values():
            lane.engine.sem_inc(lane.sem, lane.per)
    with nc.Fori(0, turns) as i:
        for t in tasks:
            for lane in t.lanes.values():
                lane.turn = i
        going = [[0, k.counts.get((t.name, "steps"), 100), t.steps(i, *t.lanes.values()), t] for t in tasks]
        done = object()
        while going:
            g = min(going, key=lambda g: g[0] / g[1])
            g[0] += 1
            if next(g[2], done) is done:
                k.seen[g[3].name, "steps"] = g[0]
                going.remove(g)
    for t in tasks:
        for lane in t.lanes.values():
            k.seen[lane.name] = max(lane.pos, 1)
            if lane.pos:
                for e in k.all_engines():
                    e.wait_ge(lane.sem, (turns + 1) * lane.pos)
        for end in t.ends:
            end(turns)


P = 128
NB, T, HID = 4, 1024, 128
N = NB * T
TILE = 512
NT = N // TILE
PITCH = TILE + 1


class Kit:

    def __init__(self, nc, ctx, counts, dram):
        self.nc, self.ctx, self.counts, self.dram, self.seen, self.drains = nc, ctx, counts, dram, {}, {}

    def sb(self, name, shape, dt=F32, ctx=None):
        return (ctx or self.ctx).enter_context(self.nc.sbuf_tensor(name, shape, dt))

    def ps(self, name, shape, ctx, dt=F32):
        return ctx.enter_context(self.nc.psum_tensor(name, shape, dt))

    def sem(self, name):
        return self.ctx.enter_context(self.nc.semaphore(name))

    def drain_sem(self, name, dmas):
        if name not in self.drains:
            self.drains[name] = (self.sem(name), dmas)
        return self.drains[name][0]

    def drained(self, engine, name, turn):
        sem, dmas = self.drains[name]
        engine.wait_ge(sem, turn * (16 * dmas) + 16 * dmas)

    def drain_over(self, name, turns):
        sem, dmas = self.drains[name]
        for e in self.all_engines():
            e.wait_ge(sem, 16 * dmas * (turns + 1))

    def all_engines(self):
        nc = self.nc
        return (nc.tensor, nc.vector, nc.scalar, nc.gpsimd, nc.sync)


def load(k, sem, total, *pairs):
    for n, (dst, src) in enumerate(pairs):
        (k.nc.sync, k.nc.scalar)[n % 2].dma_start(dst, src).then_inc(sem, 16)
        total += 16
    return total


def normalise(k, name, src, dst, w, gather, eps, centre=None, extra=None, gain=None):
    nc = k.nc
    group = 4
    with ExitStack() as c:
        wide = [k.ps(f"{name}_wide{g}", [P, TILE], c) for g in range(group)]
        var = k.ps(f"{name}_var", [P, TILE], c)
        cent = [k.sb(f"{name}_cent{g}", [P, TILE], ctx=c) for g in range(group)] if centre is not None else None
        sq = [k.sb(f"{name}_sq{g}", [P, TILE], ctx=c) for g in range(group)]
        sd = k.sb(f"{name}_sd", [P, TILE], ctx=c)
        task = Task(k, name)

        @task.body
        def _(i, pe, dve, act, pool, sp):
            centred = [None] * group
            if centre is not None:
                for g in range(group):
                    wait(nc.tensor, dve.last(f"out{g}"))
                    got = pe(nc.tensor.matmul(wide[g][:, :], centre, src(i * group + g), start=True, stop=True))
                    wait(nc.vector, got)
                    centred[g] = dve(nc.vector.tensor_tensor(cent[g][:, :], src(i * group + g), wide[g][:, :], ALU.subtract), f"cent{g}")
            wait(nc.tensor, act.last("sd"))
            for g in range(group):
                if centre is not None:
                    wait(nc.scalar, centred[g])
                wait(nc.scalar, pe.last("var"))
                squared = act(nc.scalar.activation(sq[g][:, :], cent[g][:, :] if centre is not None else src(i * group + g), ACT.Square))
                wait(nc.tensor, squared)
                got = pe(nc.tensor.matmul(var[32 * g:32 * g + 32, :], gather, sq[g][:, :], start=True, stop=True), "var")
            wait(nc.scalar, got, pe.last("spread"))
            rooted = act(nc.scalar.activation(sd[:, :], var[:, :], ACT.Sqrt, bias=eps[:, 0:1]), "sd")
            wait(nc.vector, rooted)
            inverse = dve(nc.vector.reciprocal(sd[:, :], sd[:, :]))
            for g in range(group):
                wait(nc.tensor, inverse, dve.last(f"out{g}"))
                got = pe(nc.tensor.matmul(wide[g][:, :], w("spread", g * P, (g + 1) * P), sd[:, :], start=True, stop=True), "spread")
                wait(nc.vector, got)
                what = cent[g][:, :] if centre is not None else src(i * group + g)
                if gain is None:
                    out = dve(nc.vector.tensor_tensor(dst(i * group + g), what, wide[g][:, :], ALU.mult), f"out{g}")
                else:
                    out = dve(nc.vector.scalar_tensor_tensor(dst(i * group + g), what, gain, wide[g][:, :], ALU.mult, ALU.mult), f"out{g}")
                if extra:
                    extra(i * group + g, dve, out)
            yield
        run(k, NT // group, task)


class Ring:

    def __init__(self, k, name, slots):
        self.k, self.name, self.slots, self.n, self.held = k, name, slots, 0, {}

    def take(self, engine, lanes):
        slot = self.n % len(self.slots)
        self.n += 1
        marks = self.held.get(slot)
        assert marks != ()
        if marks is None:
            before = self.k.counts.get((self.name, slot), ())
            marks = [(lanes[name], pos - lanes[name].per) for name, pos in before]
        owed[id(engine)] = (*owed.get(id(engine), ()), *marks)
        self.held[slot] = ()
        self.slot = slot
        return self.slots[slot]

    def release(self, slot, *marks):
        self.held[slot] = marks
        self.k.seen[self.name, slot] = tuple((lane.key, pos) for lane, pos in marks)


KD, NH, DK, DV = 64, 4, 16, 32
CH = 128
NC = TILE // CH
SB = 32
NJ = TILE // SB
LOW = (1, 2, 4, 8, 16)


def recurrence(k, c, w, xn, out, gate):
    nc = k.nc
    V, A, E, G = nc.vector, nc.scalar, nc.tensor, nc.gpsimd
    sb = lambda name, *shape: k.sb(f"rw_{name}", [P, *shape], ctx=c)
    banks = [k.ps(f"rw_bank{n}", [P, TILE], c) for n in range(2)]
    delta = [sb(f"delta{s}", TILE) for s in range(2)]
    mixed0 = sb("mixed0", TILE)
    low = [[sb(f"low{s}{a}", TILE) for a in range(2)] for s in range(2)]
    mix = [sb(f"mix{n}", TILE) for n in range(3)]
    hidden = [sb(f"hidden{s}", TILE) for s in range(2)]
    tanhg = hidden
    rate, key, rec = sb("rate", TILE), sb("key", TILE), sb("rec", TILE)
    val = [sb(f"val{s}", TILE) for s in range(2)]
    pre, suf = sb("pre", TILE), sb("suf", TILE)
    total = {h: sb(f"total{h}", TILE // h) for h in (2, 4, 8, 16, 32, 64, 128)}
    gr = [sb(f"gr{n}", TILE // 2) for n in range(2)]
    gl = [sb(f"gl{n}", TILE // 2) for n in range(2)]
    rr0 = sb("selves", NH * TILE)
    rr = [rr0[:, n * NH * TILE // 2:(n + 1) * NH * TILE // 2] for n in range(2)]
    kk = [sb(f"kk{n}", TILE) for n in range(2)]
    diag = sb("diag", 2, NC, NH, SB)
    full = sb("full", 2 * NC, NH, CH)
    gp, gs = sb("gp", TILE), sb("gs", TILE)
    qs, kc, kct = gp, gs, sb("kct", TILE)
    ru = gs
    decay = sb("decay", NC)
    add = sb("add", NC, CH)
    state = sb("state", NC, CH)
    carry = sb("carry", CH)
    cell = sb("cell", 1)

    def carrier(bank):
        E.matmul(bank[:, 0:1], k.bf["ident"], k.bf["ident"][:, 0:1], start=True, stop=True)

    s0 = k.sem("rw_zero")
    V.memset(full[:, :, :, :], 0.0).then_inc(s0, 1)
    V.memset(carry[:, :], 0.0).then_inc(s0, 1)
    for t in kk:
        V.memset(t[:, :], 0.0).then_inc(s0, 1)
    for e in k.all_engines():
        e.wait_ge(s0, 4)
    task = Task(k, "rw")

    @task.body
    def _(it, pe, dve, act, pool, sp):
        lanes = task.lanes
        ring = Ring(k, "rw_ring", banks)

        def take():
            b = ring.take(E, lanes)
            return ring.slot, b

        mring = Ring(k, "rw_mix", mix)
        xt = [xn[:, bass.ds((it + 4 * s) * PITCH + 1, TILE)] for s in range(2)]
        sh = [xn[:, bass.ds((it + 4 * s) * PITCH, TILE)] for s in range(2)]
        lows = [None, None]
        for s in range(2):
            d = dve(V.tensor_tensor(delta[s][:, :], sh[s], xt[s], ALU.subtract))
            wait(V, d, pe.last("low1") if s == 0 else p)
            m = dve(V.scalar_tensor_tensor(mixed0[:, :], delta[s][:, :], w("mu0"), xt[s], ALU.mult, ALU.add))
            for a in range(2):
                slot, b = take()
                wait(E, m)
                p = pe(E.matmul(b[:, :], w(f"wx0{a}"), mixed0[:, :], start=True, stop=True), f"low{s}")
                wait(A, p, pe.last(f"mus{s}"))
                t = act(A.activation(low[s][a][:, :], b[:, :], ACT.Tanh))
                ring.release(slot, t)
                yield
            lows[s] = t

        def mixtures(i):
            got = []
            for s in range(2):
                slot, b = take()
                wait(E, lows[s])
                p = pe(E.matmul(b[:, :], w(f"wx2{i}"), low[s][i // 4][:, :], start=True, stop=True), f"mus{s}")
                got.append((slot, b, p))
            yield
            mixed = []
            for s, (slot, b, p) in enumerate(got):
                m = mring.take(V, lanes)
                mslot = mring.slot
                wait(V, p)
                d = dve(V.scalar_tensor_tensor(m[:, :], b[:, :], w("xbias", i, i + 1), delta[s][:, :], ALU.add, ALU.mult))
                ring.release(slot, d)
                mixed.append((mslot, m, d))
                yield
            for s, (mslot, m, d) in enumerate(mixed):
                wait(V, d)
                mixed[s] = (mslot, m, dve(V.tensor_tensor(m[:, :], m[:, :], xt[s], ALU.add)))
            yield
            return mixed

        def halves(t, h):
            v = t[:, :].rearrange("p (n e h) -> p n e h", e=2, h=h)
            return v[:, :, 0, :], v[:, :, 1, :]

        def spread(h, odd, n, width):
            src = rate if h == 1 else total[h]
            v = src[:, :].rearrange("p (n e) -> p n e", e=2)[:, :, odd:odd + 1]
            return v.broadcast_to([P, n, width])

        def levels(h):
            g = h // 2
            n = TILE // h
            nonlocal summed
            if g == 1:
                wait(V, rated)
                pe_, po = halves(pre, 1)
                se, so = halves(suf, 1)
                re_, ro = halves(rate, 1)
                wait(V, act.last("gp"))
                V.memset(pe_, 0.0)
                V.memset(so, 0.0)
                V.tensor_copy(po, re_)
                V.tensor_copy(se, ro)
                summed = dve(V.tensor_tensor(total[2][:, :].unsqueeze(2), re_, ro, ALU.add), "rate")
            else:
                wait(V, summed, *exps)
                _, po = halves(pre, g)
                se, _ = halves(suf, g)
                dve(V.tensor_tensor(po, po, spread(g, 0, n, g), ALU.add))
                dve(V.tensor_tensor(se, se, spread(g, 1, n, g), ALU.add))
                tt = total[g][:, :].rearrange("p (n e) -> p n e", e=2)
                summed = dve(V.tensor_tensor(total[h][:, :].unsqueeze(2), tt[:, :, 0:1], tt[:, :, 1:2], ALU.add))

        def factors(li, h):
            nonlocal exps
            par = li % 2
            levels(h)
            _, po = halves(pre, h)
            se, _ = halves(suf, h)
            wait(A, summed, scaled[par])
            e1 = act(A.activation(gr[par][:, :].rearrange("p (n h) -> p n h", h=h), po, ACT.Exp, scale=-1.0))
            e2 = act(A.activation(gl[par][:, :].rearrange("p (n h) -> p n h", h=h), se, ACT.Exp, scale=-1.0))
            exps = ready[h] = (e1, e2)

        summed, exps, ready = None, (), {}
        scaled = [dve.last("scaled0"), dve.last("scaled1")]
        yield
        hs = [None, None]
        for s, (ms, m, d) in enumerate((yield from mixtures(1))):
            slot, b = take()
            wait(E, d)
            p = pe(E.matmul(b[:, :], w("ww1"), m[:, :], start=True, stop=True))
            mring.release(ms, p)
            wait(A, p, pe.last(f"rate{s}"), dve.last(f"gate{s}"))
            hs[s] = act(A.activation(hidden[s][:, :], b[:, :], ACT.Tanh))
            ring.release(slot, hs[s])
        yield

        def project(i, weight, dst, prev):
            mixed = yield from mixtures(i)
            slot, b = take()
            for s, (ms, m, d) in enumerate(mixed):
                wait(E, d)
                p = pe(E.matmul(b[64 * s:64 * s + KD, :], w(weight), m[:, :], start=True, stop=True))
                mring.release(ms, p)
            yield
            wait(A, p, *prev)
            done = act(A.activation(dst[:, :], b[:, :], ACT.Copy))
            ring.release(slot, done)
            return done

        keyed = yield from project(2, "wk", key, (dve.last("key"), pe.last("one")))
        slot, b = take()
        for s in range(2):
            wait(E, hs[s])
            p = pe(E.matmul(b[64 * s:64 * s + KD, :], w("ww2"), hidden[s][:, :], start=True, stop=True), f"rate{s}")
        hidden_read = p
        yield
        wait(A, p, dve.last("rate"))
        rated = act(A.activation(rate[:, :], b[:, :], ACT.Exp, bias=w("bw2")))
        ring.release(slot, rated)
        factors(1, 2)
        yield
        recd = yield from project(0, "wr", rec, (dve.last("rec"),))

        vals = [None, None]

        def values_and_gate():
            for s, (ms, m, d) in enumerate((yield from mixtures(3))):
                slot, b = take()
                wait(E, d)
                for n in range(NC):
                    p = E.matmul(b[:, n * CH:(n + 1) * CH], m[:, n * CH:(n + 1) * CH], w("wv"), start=True, stop=True)
                p = pe(p)
                mring.release(ms, p)
                yield
                wait(A, p, pe.last(f"out{s}"))
                vals[s] = act(A.activation(val[s][:, :], b[:, :], ACT.Copy))
                ring.release(slot, vals[s])
            for s, (ms, m, d) in enumerate((yield from mixtures(4))):
                slot, b = take()
                wait(E, d)
                p = pe(E.matmul(b[:, :], w("wg"), m[:, :], start=True, stop=True))
                mring.release(ms, p)
                wait(A, p, hidden_read)
                t = act(A.activation(tanhg[s][:, :], b[:, :], ACT.Tanh, scale=0.5))
                yield
                wait(V, t)
                d = dve(V.scalar_tensor_tensor(gate[:, bass.ds((it + 4 * s) * TILE, TILE)], tanhg[s][:, :], 1.0, b[:, :], ALU.add, ALU.mult), f"gate{s}")
                ring.release(slot, d)

        yield from values_and_gate()

        wait(V, recd, keyed, pe.last("out1"))
        d = dve(V.tensor_scalar(ru[:, :], rec[:, :], w("bonus"), None, ALU.mult))
        wait(V, d, pe.last("self"), pe.last("read0"), pe.last("read1"))
        for h in range(NH):
            src = ru[:, :].rearrange("p (j t) -> p j t", t=SB)
            dst = rr0[:, :].rearrange("p (j h t) -> p j h t", h=NH, t=SB)[:, :, h, :]
            selfr = dve(V.tensor_scalar(dst, src, w("headmask", h, h + 1), None, ALU.mult))
            yield

        def blocks(keys, recs, width, ready, name):
            made_ = []
            for s in range(2):
                slot, b = take()
                wait(E, *ready)
                carrier(b)
                for j in range(NJ):
                    cc, q = divmod(j, CH // SB)
                    p = E.matmul(b[SB * q:SB * q + SB, cc * NH * width:(cc + 1) * NH * width],
                                 keys[64 * s:64 * s + KD, SB * j:SB * j + SB],
                                 recs[64 * s:64 * s + KD, j * NH * width:(j + 1) * NH * width],
                                 start=True, stop=True)
                made_.append((s, slot, b, pe(p, name if s == 1 else None)))
                yield
            return made_

        for s, slot, b, p in (yield from blocks(key, rr0, SB, (selfr,), "self")):
            wait(V, p, act.last("full"), dve.last("full"))
            placed = dve(V.tensor_tensor(diag[:, s, :, :, :].rearrange("p c h t -> p (c h) t"),
                                         b[:, :].rearrange("p (n t) -> p n t", t=SB),
                                         w("eye32").unsqueeze(1).broadcast_to([P, NC * NH, SB]), ALU.mult))
            ring.release(slot, placed)

        selves_read = p

        def place(h, products):
            nonlocal placed
            for s, slot, b, p in products:
                if h <= 16:
                    mask = w(f"mask{h}").bitcast(U32).unsqueeze(1).broadcast_to([P, NC * NH, 16])
                    wait(V, p, placed)
                    V.memset(cell[:, :], 0.0)
                    o = diag[:, s, :, :, :].rearrange("p c h (n e t) -> p (c h) n e t", e=2, t=h)[:, :, :, 1, :]
                    placed = dve(V.copy_predicated(o, mask.rearrange("p c (n t) -> p c n t", t=h),
                                                   b[:, 0:NC * NH * 16].rearrange("p (c n t) -> p c n t", n=16 // h, t=h)))
                    ring.release(slot, placed)
                    yield
                else:
                    wait(A, p, pe.last(f"out{s}"))
                    for q in range(2):
                        rows = slice(64 * q, 64 * q + 32)
                        d = act(A.activation(full[rows, NC * s:NC * s + NC, :, 64 * q + 32:64 * q + 64].rearrange("p c h t -> p (c h) t"),
                                             b[rows, :].rearrange("p (n t) -> p n t", t=32), ACT.Copy))
                    ring.release(slot, d)
                    yield

        read = [None, None]
        pending = None
        for li, h in enumerate((1, 2, 4, 8, 16, 32, 64)):
            n = TILE // (2 * h)
            par = li % 2
            R, K_ = rr[par], kk[par]
            if h in (4, 16, 64):
                factors(li, h)
                if h < 64:
                    factors(li + 1, 2 * h)
                else:
                    levels(CH)
                    wait(A, summed, pe.last("out1"), dve.last("state"))
                    act(A.activation(gp[:, :], pre[:, :], ACT.Exp, scale=-1.0))
                    act(A.activation(gs[:, :], suf[:, :], ACT.Exp, scale=-1.0), "gp")
                    decayed = act(A.activation(decay[:, :], total[CH][:, :], ACT.Exp, scale=-1.0))
                yield
            wait(V, *ready.get(h, ()))
            wait(V, read[par]) if li > 1 else wait(V, selves_read)
            rodd = halves(rec, h)[1]
            keven = halves(key, h)[0]
            if h <= 16:
                rv = R[:, :].rearrange("p (j h n t) -> p j h n t", h=NH, n=16 // h, t=h)
                dst = [rv[:, :, a, :, :] for a in range(NH)]
                ro = rodd.rearrange("p (j n) h -> p j n h", n=16 // h)
                gg = gr[par][:, :].rearrange("p (j n h) -> p j n h", n=16 // h, h=h)
            else:
                rv = R[:, :].rearrange("p (j h t) -> p j h t", h=NH, t=h)
                dst = [rv[:, :, a, :] for a in range(NH)]
                ro, gg = rodd, gr[par][:, :].rearrange("p (n h) -> p n h", h=h)
            for a in range(NH):
                if h == 1:
                    made = dve(V.tensor_scalar(dst[a], ro, w("headmask", a, a + 1), None, ALU.mult))
                else:
                    made = dve(V.scalar_tensor_tensor(dst[a], gg, w("headmask", a, a + 1), ro, ALU.mult, ALU.mult))
                yield
            if h > 1:
                ke = halves(K_, h)[0]
                made = dve(V.tensor_tensor(ke, gl[par][:, :].rearrange("p (n h) -> p n h", h=h), keven, ALU.mult), f"scaled{par}")
                scaled[par] = made
            yield
            if pending:
                yield from place(*pending)
                pending = None
            if h <= 16:
                products = yield from blocks(key if h == 1 else K_, R, 16, (made,), f"read{par}")
                read[par] = products[1][3]
                if h == 1:
                    k.seen["rw_pe", "one"] = read[par][1]
                pending = (h, products)
            elif h == 32:
                products = []
                for s in range(2):
                    slot, b = take()
                    wait(E, made)
                    carrier(b)
                    for n2 in range(2 * NC):
                        cc, q = divmod(n2, 2)
                        p = E.matmul(b[64 * q:64 * q + 32, cc * 128:cc * 128 + 128],
                                     K_[64 * s:64 * s + KD, 64 * n2:64 * n2 + 32],
                                     R[64 * s:64 * s + KD, n2 * 128:(n2 + 1) * 128], start=True, stop=True)
                    p = pe(p, f"read{par}")
                    products.append((s, slot, b, p))
                    yield
                read[par] = p
                pending = (h, products)
            else:
                for s in range(2):
                    for half in range(2):
                        slot, b = take()
                        wait(E, made)
                        carrier(b)
                        for n2 in range(2):
                            cc = 2 * half + n2
                            p = E.matmul(b[0:64, n2 * 256:n2 * 256 + 256],
                                         K_[64 * s:64 * s + KD, CH * cc:CH * cc + 64],
                                         R[64 * s:64 * s + KD, cc * 256:(cc + 1) * 256], start=True, stop=True)
                        p = pe(p, f"read{par}")
                        yield
                        wait(A, p, pe.last(f"out{s}"))
                        d = act(A.activation(full[0:64, NC * s + 2 * half:NC * s + 2 * half + 2, :, 64:128].rearrange("p c h t -> p (c h) t"),
                                             b[0:64, :].rearrange("p (n t) -> p n t", t=64), ACT.Copy))
                        ring.release(slot, d)
                read[par] = p
                offdiag = d
        wait(A, placed)
        wait(V, placed, pe.last("out1"))
        for q in range(4):
            rows = slice(SB * q, SB * q + SB)
            dst = full[rows, :, :, SB * q:SB * q + SB].rearrange("p n h t -> p (n h) t")
            src = diag[rows, :, :, :, :].rearrange("p s c h t -> p (s c h) t")
            if q % 2:
                filled_a = act(A.activation(dst, src, ACT.Copy), "full")
            else:
                filled_v = dve(V.tensor_copy(dst, src), "full")
        yield
        wait(V, decayed)
        dve(V.tensor_tensor(qs[:, :], gp[:, :], rec[:, :], ALU.mult), "rec")
        d = dve(V.tensor_tensor(kc[:, :], gs[:, :], key[:, :], ALU.mult), "key")
        k.seen["rw_dve", "gp"] = d[1]
        yield
        slot, b = take()
        wait(E, d)
        for n in range(NC):
            p = E.transpose(b[:, n * CH:(n + 1) * CH], kc[:, n * CH:(n + 1) * CH], w("ident"))
        p = pe(p)
        yield
        wait(A, p, pe.last("add"))
        t = act(A.activation(kct[:, :], b[:, :], ACT.Copy))
        ring.release(slot, t)
        yield
        slot, b = take()
        wait(E, t)
        for s in range(2):
            wait(E, vals[s])
            for n in range(NC):
                p = E.matmul(b[64 * s:64 * s + KD, n * CH:(n + 1) * CH], kct[:, n * CH + 64 * s:n * CH + 64 * s + KD],
                             val[s][:, n * CH:(n + 1) * CH], start=True, stop=True)
        p = pe(p, "add")
        yield
        wait(V, p)
        masked = dve(V.tensor_tensor(add[:, :, :], b[:, :].rearrange("p (c d) -> p c d", d=CH),
                                     w("statemask").unsqueeze(1).broadcast_to([P, NC, CH]), ALU.mult))
        ring.release(slot, masked)
        wait(V, dve.last("state"))
        st = dve(V.tensor_scalar(state[:, 0, :], carry[:, :], k.w_at("carries", it), None, ALU.mult))
        for n in range(NC):
            wait(V, masked, st)
            dst = state[:, n + 1, :] if n + 1 < NC else carry[:, :]
            st = dve(V.scalar_tensor_tensor(dst, state[:, n, :], decay[:, n:n + 1], add[:, n, :], ALU.mult, ALU.add), "state")
        yield
        for s in range(2):
            slot, b = take()
            wait(E, st, filled_a, filled_v, offdiag, vals[s])
            for n in range(NC):
                cols = slice(n * CH, (n + 1) * CH)
                E.matmul(b[:, cols], state[64 * s:64 * s + KD, n, :], qs[64 * s:64 * s + KD, cols], start=True, stop=True)
                for h in range(NH):
                    p = E.matmul(b[DV * h:DV * h + DV, cols], val[s][:, n * CH + DV * h:n * CH + DV * h + DV],
                                 full[:, NC * s + n, h, :], start=False, stop=True, skip_group_check=True)
            p = pe(p, f"out{s}")
            yield
            wait(A, p)
            d = act(A.activation(out[:, bass.ds((it + 4 * s) * PITCH + 1, TILE)], b[:, :], ACT.Copy))
            ring.release(slot, d)
    return task


def recurrence_out(k, w, y, gate, x):
    nc = k.nc
    V, A, E = nc.vector, nc.scalar, nc.tensor
    with ExitStack() as c:
        scaled = [k.sb(f"go_scaled{g}", [P, TILE], ctx=c) for g in range(2)]
        gated = [k.sb(f"go_gated{g}", [P, TILE], ctx=c) for g in range(2)]
        bank = [k.ps(f"go_bank{g}", [P, TILE], c) for g in range(2)]
        task = Task(k, "go")

        @task.body
        def _(i, pe, dve, act, pool, sp):
            for g in range(2):
                cols = bass.ds((2 * i + g) * TILE, TILE)
                wait(A, dve.last(f"gated{g}"))
                a = act(A.activation(scaled[g][:, :], y[:, bass.ds((2 * i + g) * PITCH + 1, TILE)], ACT.Identity, scale=w("gnw"), bias=w("gnb")))
                wait(V, a, pe.last(f"proj{g}"))
                d = dve(V.scalar_tensor_tensor(gated[g][:, :], scaled[g][:, :], 0.5, gate[:, cols], ALU.mult, ALU.mult), f"gated{g}")
                wait(E, d, dve.last(f"sum{g}"))
                p = pe(E.matmul(bank[g][:, :], w("wo"), gated[g][:, :], start=True, stop=True), f"proj{g}")
            for g in range(2):
                cols = bass.ds((2 * i + g) * TILE, TILE)
                wait(V, (pe, g + 1))
                dve(V.tensor_tensor(x[:, cols], bank[g][:, :], x[:, cols], ALU.add), f"sum{g}")
            yield

        run(k, NT // 2, task)


class Arrivals:

    def __init__(self, k, name, slots, lane):
        self.k, self.name, self.slots, self.lane = k, name, slots, lane
        self.sems = [k.sem(f"{name}{n}") for n in range(len(slots))]
        self.fills = [0] * len(slots)

    def started(self, slot, dma):
        dma.then_inc(self.sems[slot], 16)
        self.fills[slot] += 1
        self.k.seen[self.name, slot, "fills"] = self.fills[slot]
        return slot, self.fills[slot]

    def wait(self, engine, landed):
        slot, n = landed
        per = self.k.counts.get((self.name, slot, "fills"), 1)
        engine.wait_ge(self.sems[slot], self.lane.turn * (16 * per) + 16 * n)

    def end(self, turns):
        for e in self.k.all_engines():
            for sem, fills in zip(self.sems, self.fills):
                if fills:
                    e.wait_ge(sem, 16 * fills * turns)


FH, FE, FI, FD = 8, 16, 64, 16
EP = FE // 2
TERMS = 6
ACT_PARTS = (0, 0, 1, 1, 0, 2)
WEIGHT_PARTS = (0, 1, 0, 1, 2, 0)


def split3(V, lane, src, parts, rest):
    hi, mid, lo = parts
    d = lane(V.tensor_copy(hi, src))
    wait(V, d)
    d = lane(V.tensor_tensor(rest, src, hi, ALU.subtract))
    wait(V, d)
    d = lane(V.tensor_copy(mid, rest))
    wait(V, d)
    return lane(V.tensor_tensor(lo, rest, mid, ALU.subtract))


def top2(k, w, V, A, dve, act, logits, groups, ne, t, weights_of_softmax):
    G3 = [P, groups, ne]
    wide = lambda name: t[name][:, :].unsqueeze(2).broadcast_to(G3)
    order = w("descending", 0, ne).unsqueeze(1).broadcast_to(G3)
    v = lambda name: t[name][:, :].rearrange("p (g e) -> p g e", e=ne)

    def first(src, peak, onehot, ready):
        wait(V, *ready)
        d = dve(V.tensor_reduce(t[peak][:, :], src, AX, ALU.max))
        yield
        wait(V, d)
        d = dve(V.tensor_tensor(v("eq"), src, wide(peak), ALU.is_ge))
        yield
        wait(V, d)
        d = dve(V.tensor_tensor(v("eq"), v("eq"), order, ALU.mult))
        yield
        wait(V, d)
        d = dve(V.tensor_reduce(t["place"][:, :], v("eq"), AX, ALU.max))
        yield
        wait(V, d)
        return dve(V.tensor_tensor(v(onehot), order, wide("place"), ALU.is_equal))

    d1 = yield from first(logits, "peak", "one", ())
    wait(V, d1)
    d = dve(V.scalar_tensor_tensor(v("rest"), v("one"), -3e38, logits, ALU.mult, ALU.add))
    off = dve(V.tensor_tensor(v("soft"), logits, wide("peak"), ALU.subtract))
    wait(A, off)
    e = act(A.activation(t["soft"][:, :], t["soft"][:, :], ACT.Exp))
    d2 = yield from first(v("rest"), "peak2", "two", (d,))
    yield
    wait(V, d2)
    d = dve(V.tensor_tensor(v("one"), v("one"), v("two"), ALU.add))
    yield
    wait(V, d, e)
    chosen = dve(V.tensor_tensor(v("one"), v("one"), v("soft"), ALU.mult))
    if weights_of_softmax:
        d = dve(V.tensor_reduce(t["sum"][:, :], v("soft"), AX, ALU.add))
        wait(V, d)
    else:
        d = dve(V.tensor_reduce(t["sum"][:, :], v("soft"), AX, ALU.add))
        wait(V, chosen)
        d2 = dve(V.tensor_reduce(t["place"][:, :], v("one"), AX, ALU.add))
        wait(V, d, d2)
        d = dve(V.scalar_tensor_tensor(t["sum"][:, :], t["sum"][:, :], 1e-9, t["place"][:, :], ALU.mult, ALU.add))
        wait(V, d)
    d = dve(V.reciprocal(t["sum"][:, :], t["sum"][:, :]))
    wait(V, d, chosen)
    return v, wide, d


def moe0_prepare(k, c, w, xn, stack, shares, tag, first):
    nc = k.nc
    G = nc.gpsimd
    V, A, E, S = nc.vector, nc.scalar, nc.tensor, nc.sync
    sb = lambda name, *shape, dt=F32: k.sb(f"{tag}_{name}", [P, *shape], dt, ctx=c)
    banks = [k.ps(f"{tag}_bank{n}", [P, TILE], c) for n in range(3)]
    h, rest, sharesT = sb("h", TILE), sb("resth", TILE), sb("sharesT", TILE)
    parts = [sb(f"part{n}", TILE, dt=BF16) for n in range(3)]
    logits = sb("logits", TILE)
    groups = TILE // FE
    t = {n: sb(n, TILE) for n in ("eq", "one", "two", "rest", "soft", "cw")}
    t |= {n: sb(n, groups) for n in ("peak", "peak2", "place", "sum")}
    for name, n in ((f"{tag}_parts", TERMS), (f"{tag}_shares", 1)):
        S.sem_inc(k.drain_sem(name, n), 16 * n)
    task = Task(k, tag)

    @task.body
    def _(turn, pe, dve, act, pool, sp):
        i = 2 * turn + first
        wait(E, act.last("h"))
        p = pe(E.matmul(banks[0][:, :], w("wm"), xn[:, bass.ds(i * PITCH + 1, TILE)], start=True, stop=True))
        wait(A, p, pool.last("split"), pe.last("logits"))
        hd = act(A.activation(h[:, :], banks[0][:, :], ACT.Identity, bias=w("bm")), "h")
        yield
        wait(E, hd, act.last("logits"))
        for n in range(NC):
            p = E.matmul(banks[1][:, n * CH:(n + 1) * CH], h[:, n * CH:(n + 1) * CH], w("emb"), start=True, stop=True)
        p = pe(p, "logits")
        wait(A, p, dve.last("topk"))
        lg = act(A.activation(logits[:, :], banks[1][:, :], ACT.Copy), "logits")
        k.drained(A, f"{tag}_parts", turn)
        wait(A, hd)
        hi = act(A.activation(parts[0][:, :], h[:, :], ACT.Copy))
        wait(G, hi)
        r = pool(G.tensor_tensor(rest[:, :], h[:, :], parts[0][:, :], ALU.subtract))
        yield
        wait(A, r)
        mid = act(A.activation(parts[1][:, :], rest[:, :], ACT.Copy))
        yield
        wait(G, mid)
        pool(G.tensor_tensor(parts[2][:, :], rest[:, :], parts[1][:, :], ALU.subtract))
        k.seen[f"{tag}_pool", "split"] = pool.pos
        for n in range(TERMS):
            wait(S, (pool, pool.pos))
            dst = stack[bass.ds(i, 1), :, n * FD:(n + 1) * FD, :].rearrange("a h d t -> (a h) d t")
            S.dma_start(dst, parts[ACT_PARTS[n]][:, :]).then_inc(k.drain_sem(f"{tag}_parts", TERMS), 16)
        wait(V, lg)
        yield
        v, wide, inv = yield from top2(k, w, V, A, dve, act, logits[:, :].rearrange("p (g e) -> p g e", e=FE), groups, FE, t, True)
        wait(V, pe.last("turned"))
        cw = dve(V.tensor_tensor(v("cw"), v("one"), wide("sum"), ALU.mult), "topk")
        wait(E, cw, act.last("shares"))
        for n in range(NC):
            p = E.transpose(banks[2][:, n * CH:(n + 1) * CH], t["cw"][:, n * CH:(n + 1) * CH], w("ident"))
        p = pe(p, "turned")
        k.drained(A, f"{tag}_shares", turn)
        wait(A, p)
        a = act(A.activation(sharesT[:, :], banks[2][:, :], ACT.Copy), "shares")
        wait(S, a)
        S.dma_start(shares[bass.ds(i, 1), :, :].rearrange("a q t -> (a q) t"), sharesT[:, :]).then_inc(k.drain_sem(f"{tag}_shares", 1), 16)
        yield

    for name in (f"{tag}_parts", f"{tag}_shares"):
        task.ends.append(lambda turns, name=name: k.drain_over(name, turns))
    return task


def moe0_weights(k, c, w, w1s):
    G, S = k.nc.gpsimd, k.nc.sync
    rows = TERMS * FD
    w1f = k.sb("mw_w1f", [rows, FE * FI], ctx=c)
    rest = k.sb("mw_rest", [rows, FE * FI], ctx=c)
    parts = [k.sb(f"mw_part{n}", [rows, FE * FI], BF16, ctx=c) for n in range(3)]
    got, made = k.sem("mw_got"), k.sem("mw_made")
    S.dma_start(w1f[:, :], k.dram["w1"]).then_inc(got, 16)
    G.wait_ge(got, 16)
    count = [0]

    def step(ins):
        count[0] += 1
        ins.then_inc(made, 1)
        G.wait_ge(made, count[0])

    step(G.tensor_copy(parts[0][:, :], w1f[:, :]))
    step(G.tensor_tensor(rest[:, :], w1f[:, :], parts[0][:, :], ALU.subtract))
    step(G.tensor_copy(parts[1][:, :], rest[:, :]))
    step(G.tensor_tensor(parts[2][:, :], rest[:, :], parts[1][:, :], ALU.subtract))
    for n in range(3):
        step(G.tensor_scalar(parts[n][:, :], parts[n][:, :], w(f"rows{n}")[0:rows], None, ALU.mult))
    step(G.tensor_tensor(rest[:, :], parts[0][:, :], parts[1][:, :], ALU.add))
    step(G.tensor_tensor(w1s[:, :], rest[:, :], parts[2][:, :], ALU.add))

    def ready():
        for e in k.all_engines():
            e.wait_ge(made, count[0])
    return ready


def moe0(k, c, w, w1s, stack, shares, x):
    nc = k.nc
    V, A, E, S, G = nc.vector, nc.scalar, nc.tensor, nc.sync, nc.gpsimd
    sb = lambda name, *shape, dt=F32: k.sb(f"m0_{name}", shape, dt, ctx=c)
    up = [k.ps(f"m0_up{n}", [P, TILE], c) for n in range(3)]
    down = [k.ps(f"m0_down{n}", [P, TILE], c) for n in range(2)]
    sums = k.ps("m0_sums", [P, TILE], c)
    terms = sb("terms", TERMS * FD, 4, TILE, dt=BF16)
    share = sb("share", P, 4, TILE)
    act_h = sb("act_h", P, 2, 4, 2, TILE)
    prod = [sb(f"prod{n}", P, TILE) for n in range(4)]
    task = Task(k, "m0")

    @task.body
    def _(turn, pe, dve, act, pool, sp):
        lanes = task.lanes
        tring, sring = Ring(k, "m0_tring", list(range(4))), Ring(k, "m0_sring", list(range(4)))
        tarr = Arrivals(k, "m0_tarr", list(range(4)), sp)
        sarr = Arrivals(k, "m0_sarr", list(range(4)), sp)
        task.ends += [tarr.end, sarr.end]
        upring = Ring(k, "m0_upring", up)
        dring = Ring(k, "m0_dring", down)
        pring = Ring(k, "m0_pring", prod)
        hring = Ring(k, "m0_hring", list(range(2)))
        units = [(u, hp, half) for u in range(2) for hp in range(4) for half in range(2)]
        got, shared, act_of = {}, {}, {}

        def fetch(n):
            if n >= len(units):
                return
            u, hp, half = units[n]
            i = 2 * turn + u
            for j in range(2):
                hd = 2 * hp + j
                if half == 0:
                    slot = tring.take(S, lanes)
                    wait(S)
                    src = stack[bass.ds(i, 1), hd, :, :].rearrange("a r t -> (a r) t")
                    got[u, hd] = tarr.started(slot, S.dma_start(terms[:, slot, :], src))
                slot = sring.take(S, lanes)
                wait(S)
                rows = shares[bass.ds(i, 1), hd * FE + half * 8:hd * FE + half * 8 + 8, :].rearrange("a e t -> (a e) t")
                src = rows.unsqueeze(1).broadcast_to([8, FD, TILE])
                shared[u, hd, half] = sarr.started(slot, S.dma_start(share[:, slot, :], src))

        def ups(u, hp, half, e):
            ep = 4 * half + e
            for j in range(2):
                b = upring.take(E, lanes)
                uslot = upring.slot
                if e == 0 and half == 0:
                    tarr.wait(E, got[u, 2 * hp + j])
                wait(E)
                slot = got[u, 2 * hp + j][0]
                p = pe(E.matmul(b[:, :], w1s[:, ep * P:(ep + 1) * P], terms[:, slot, :], start=True, stop=True))
                if e == 3 and half == 1:
                    tring.release(slot, p)
                if e == 0 and j == 0:
                    hring.take(A, lanes)
                    act_of[u, hp, half] = hring.slot
                wait(A, p)
                a = act(A.activation(act_h[:, act_of[u, hp, half], e, j, :], b[:, :], ACT.Gelu, bias=w("b1", ep, ep + 1)))
                upring.release(uslot, a)
                yield
            return a

        def downs(u, hp, half, ready):
            hslot = act_of[u, hp, half]
            folds = []
            for j in range(2):
                hd = 2 * hp + j
                d = dring.take(E, lanes)
                dslot = dring.slot
                wait(E, ready)
                for e in range(4):
                    ep = 4 * half + e
                    p = E.matmul(d[32 * e:32 * e + 32, :], w("w2", 32 * ep, 32 * ep + 32), act_h[:, hslot, e, j, :], start=True, stop=True)
                p = pe(p)
                if j == 1:
                    hring.release(hslot, p)
                pr = pring.take(V, lanes)
                pslot = pring.slot
                landed = shared[u, hd, half]
                sarr.wait(V, landed)
                wait(V, p)
                v = dve(V.scalar_tensor_tensor(pr[:, :], d[:, :], w("b2", half, half + 1), share[:, landed[0], :], ALU.add, ALU.mult))
                dring.release(dslot, v)
                sring.release(landed[0], v)
                if half == 0:
                    first[j] = pr, pslot, v
                else:
                    pr0, pslot0, v0 = first[j]
                    wait(G, v0, v)
                    g = pool(G.tensor_tensor(pr0[:, :], pr0[:, :], pr[:, :], ALU.add))
                    pring.release(pslot, g)
                    folds.append((u, hd, pr0, pslot0, g))
                yield
            return folds

        def fold(folds):
            for u, hd, pr, pslot, ready in folds:
                if hd == 0:
                    wait(E, x_read[0])
                wait(E, ready)
                p = pe(E.matmul(sums[:, :], w("wo0", hd * HID, (hd + 1) * HID), pr[:, :], start=hd == 0, stop=hd == FH - 1))
                pring.release(pslot, p)
                if hd == FH - 1:
                    xc = x[:, bass.ds((2 * turn + u) * TILE, TILE)]
                    wait(V, p)
                    x_read[0] = dve(V.scalar_tensor_tensor(xc, sums[:, :], w("bo"), xc, ALU.add, ALU.add), "x")
                yield

        x_read = [dve.last("x")]
        first = [None, None]
        later, folding = None, None
        for n in range(2):
            fetch(n)
        for n, unit in enumerate(units):
            for e in range(4):
                a = yield from ups(*unit, e)
                if e == 3 and folding:
                    yield from fold(folding)
                    folding = None
                if e == 1 and later:
                    folding = yield from downs(*later)
                    later = None
                    fetch(n + 1)
            later = (*unit, a)
        yield from fold(folding)
        folding = yield from downs(*later)
        yield from fold(folding)
    return task


AH, AD = 16, 8
HG = 4
NG = AH // HG
QB = T // CH
SROWS = 96
MROW = 64
VW = 32
SCALE = AD ** -0.5


def attention_prepare(k, c, cbank, w, xn, qstack, kstack, vstack, half):
    nc = k.nc
    V, A, E, S = nc.vector, nc.scalar, nc.tensor, nc.sync
    tag = f"ap{half}"
    sb = lambda name, *shape, dt=F32: k.sb(f"{tag}_{name}", [P, *shape], dt, ctx=c)
    banks = [k.ps(f"{tag}_bank{n}", [P, TILE], cbank) for n in range(4)]
    latent, rest = sb("latent", TILE), sb("resta", TILE)
    full = {"q": sb("q", TILE), "k": sb("k", TILE)}
    parts = {n: [sb(f"{n}part{m}", TILE, dt=BF16) for m in range(3)] for n in "qk"}
    values = sb("values", NC, VW)
    dmas = {f"{tag}_q": TERMS, f"{tag}_k": TERMS, f"{tag}_v": 1}
    for name, n in dmas.items():
        S.sem_inc(k.drain_sem(name, n), 16 * n)
    task = Task(k, tag)

    @task.body
    def _(b, pe, dve, act, pool, sp):
        def send(name, dst, src):
            S.dma_start(dst, src).then_inc(k.drain_sem(name, 0), 16)

        cols = bass.ds((2 * b + half) * TILE, TILE)
        wait(E, act.last("latent"))
        p = pe(E.matmul(banks[0][:, :], w("wdown"), xn[:, cols], start=True, stop=True))
        wait(A, p, pe.last("values"))
        lat = act(A.activation(latent[:, :], banks[0][:, :], ACT.Copy), "latent")
        yield
        copied = {}
        for name, rows, bank in (("q", P, banks[1]), ("k", 32, banks[2])):
            wait(E, lat, act.last(name))
            p = pe(E.matmul(bank[0:rows, :], w(f"w{name}up"), latent[:, :], start=True, stop=True))
            wait(A, p, dve.last(f"split{name}"))
            copied[name] = act(A.activation(full[name][0:rows, :], bank[0:rows, :], ACT.Copy), name)
            yield
        wait(E, dve.last("values"))
        for n in range(NC):
            p = E.matmul(banks[3][:, n * VW:(n + 1) * VW], latent[:, n * CH:(n + 1) * CH], w("wvup"), start=True, stop=True)
        p = pe(p, "values")
        for name, rows, src in (("q", P, ACT_PARTS), ("k", 32, WEIGHT_PARTS)):
            k.drained(V, f"{tag}_{name}", b)
            wait(V, copied[name])
            d = split3(V, dve, full[name][0:rows, :], [q[0:rows, :] for q in parts[name]], rest[0:rows, :])
            k.seen[f"{tag}_dve", f"split{name}"] = d[1]
            yield
            wait(S, d)
            for m in range(TERMS):
                rows_ = slice(m * AD, (m + 1) * AD)
                if name == "q":
                    dst = qstack[bass.ds(b, 1), :, rows_, half * TILE:(half + 1) * TILE].rearrange("a h d t -> (a h) d t")
                    send(f"{tag}_q", dst, parts["q"][src[m]][:, :])
                else:
                    dst = kstack[bass.ds(b, 1), :, rows_, half * TILE:(half + 1) * TILE].rearrange("a g d t -> d (a g) t")
                    send(f"{tag}_k", dst, parts["k"][src[m]][0:AD, :].unsqueeze(1).broadcast_to([AD, NG, TILE]))
        k.drained(V, f"{tag}_v", b)
        wait(V, p)
        valued = dve(V.tensor_tensor(values[:, :, :], banks[3][:, 0:NC * VW].rearrange("p (n v) -> p n v", v=VW),
                                     w("sumcolumn").unsqueeze(1).broadcast_to([P, NC, VW]), ALU.add), "values")
        wait(S, valued)
        dst = vstack[bass.ds(b, 1), :, :, half * NC * VW:(half + 1) * NC * VW].rearrange("a g p v -> p (a g) v")
        send(f"{tag}_v", dst, values[:, :, :].rearrange("p n v -> p (n v)").unsqueeze(1).broadcast_to([P, NG, NC * VW]))
        yield

    task.drained = lambda: [k.drain_over(name, NB) for name in dmas]
    return task


def attention_max(k, c, w, qstack, kstack, maxima):
    nc = k.nc
    V, A, E, S = nc.vector, nc.scalar, nc.tensor, nc.sync
    sb = lambda name, *shape, dt=F32: k.sb(f"am_{name}", [P, *shape], dt, ctx=c)
    score = [k.ps(f"am_score{n}", [P, TILE], c) for n in range(4)]
    qs, ks = sb("qs", 2, HG, T, dt=BF16), sb("ks", 2, T, dt=BF16)
    peaks, top, rest = sb("peaks", HG, QB, 2), sb("top", HG * QB), sb("restm", CH)
    rows = sb("rows", CH)
    parts = [sb(f"part{n}", CH, dt=BF16) for n in range(3)]
    zero = k.sem("am_zero")
    V.memset(qs[:, :, :, :], 0.0).then_inc(zero, 1)
    V.memset(ks[:, :, :], 0.0).then_inc(zero, 1)
    V.memset(peaks[:, :, :, :], -3e38).then_inc(zero, 1)
    for e in k.all_engines():
        e.wait_ge(zero, 3)
    S.sem_inc(k.drain_sem("am_max", 3 * 2), 16 * 6)
    task = Task(k, "am")

    @task.body
    def _(i, pe, dve, act, pool, sp):
        lanes = task.lanes
        ring = Ring(k, "am_ring", score)
        qring, qarr = Ring(k, "am_qring", [0, 1]), Arrivals(k, "am_qarr", [0, 1], sp)
        karr = Arrivals(k, "am_karr", [0, 1], sp)
        task.ends += [qarr.end, karr.end]
        fetched = []
        for u in range(2):
            slot = qring.take(S, lanes)
            wait(S)
            src = qstack.rearrange("b (g a) r t -> (b g) r a t", a=HG)[bass.ds(2 * i + u, 1)].rearrange("x r a t -> (x r) a t")
            q = qarr.started(slot, S.dma_start(qs[0:TERMS * AD, slot, :, :], src))
            src = kstack.rearrange("b g r t -> (b g) r t")[bass.ds(2 * i + u, 1)].rearrange("x r t -> (x r) t")
            kk = karr.started(slot, S.dma_start(ks[0:TERMS * AD, slot, :], src))
            fetched.append((slot, q, kk))
        for u in range(2):
            slot, q, kk = fetched[u]
            qarr.wait(E, q)
            karr.wait(E, kk)
            reduced = None
            for blk in range(QB):
                for seg in range(blk // 4 + 1):
                    n = min(TILE, (blk + 1) * CH - seg * TILE)
                    for h in range(HG):
                        t = ring.take(E, lanes)
                        rslot = ring.slot
                        wait(E)
                        p = E.matmul(t[:, 0:n], qs[0:SROWS, slot, h, blk * CH:(blk + 1) * CH],
                                     ks[0:SROWS, slot, seg * TILE:seg * TILE + n], start=True, stop=True)
                        if seg == blk // 4:
                            p = E.matmul(t[:, n - CH:n], k.bf["ident"], k.bf["later_s"],
                                         start=False, stop=True, skip_group_check=True)
                        p = pe(p)
                        wait(V, p, dve.last("top") if u == 0 else topped)
                        reduced = dve(V.tensor_reduce(peaks[:, h, blk, seg:seg + 1], t[:, 0:n], AX, ALU.max))
                        ring.release(rslot, reduced)
                        yield
            qring.release(slot, p)
            wait(V, reduced, pe.last("turn") if u == 0 else turned_by)
            topped = dve(V.tensor_reduce(top[:, :], peaks[:, :, :, :].rearrange("p a q s -> p (a q) s"), AX, ALU.max, negate=True), "top")
            yield
            turned = ring.take(E, lanes)
            rslot = ring.slot
            wait(E, topped)
            turned_by = pe(E.transpose(turned[0:HG * QB, 0:CH], top[:, :], w("ident")), "turn")
            yield
            wait(V, turned_by)
            nr = HG * QB
            V.wait_ge(k.drain_sem("am_max", 0), i * (16 * 6) + 16 * (6 + 3 * u))
            rowed = dve(V.tensor_copy(rows[0:nr, :], turned[0:nr, 0:CH]), "rows")
            ring.release(rslot, rowed)
            yield
            wait(V, rowed)
            d = split3(V, dve, rows[0:nr, :], [q_[0:nr, :] for q_ in parts], rest[0:nr, :])
            yield
            wait(A, d)
            for m in range(3):
                dst = maxima[bass.ds(2 * i + u, 1), m, :].rearrange("x (q t) -> (x q) t", t=CH)
                A.dma_start(dst, parts[m][0:nr, :]).then_inc(k.drain_sem("am_max", 0), 16)
    task.ends.append(lambda turns: k.drain_over("am_max", turns))
    return task


def attention_sum(k, c, w, qstack, kstack, vstack, maxima, y):
    nc = k.nc
    V, A, E, S = nc.vector, nc.scalar, nc.tensor, nc.sync
    sb = lambda name, *shape, dt=F32: k.sb(f"ax_{name}", [P, *shape], dt, ctx=c)
    score = [k.ps(f"ax_score{n}", [P, TILE], c) for n in range(3)]
    sums = [k.ps("ax_sums", [P, TILE], c)]
    qs, ks = sb("qs", 2, HG, T, dt=BF16), sb("ks", 2, T, dt=BF16)
    vs = sb("vs", 2, QB, VW)
    prob = sb("prob", 2, HG, TILE)
    zero = k.sem("ax_zero")
    V.memset(qs[:, :, :, :], 0.0).then_inc(zero, 1)
    V.memset(ks[:, :, :], 0.0).then_inc(zero, 1)
    V.wait_ge(zero, 2)
    V.memset(ks[MROW:MROW + 3, :, :], 1.0).then_inc(zero, 1)
    for e in k.all_engines():
        e.wait_ge(zero, 3)
    task = Task(k, "ax")

    @task.body
    def _(i, pe, dve, act, pool, sp):
        lanes = task.lanes
        ring, sring, pring = Ring(k, "ax_ring", score), Ring(k, "ax_sring", sums), Ring(k, "ax_pring", [0, 1])
        qring = Ring(k, "ax_qring", [0, 1])
        arr = [Arrivals(k, f"ax_{n}arr", [0, 1], sp) for n in "qkvm"]
        task.ends += [a.end for a in arr]
        fetched = []
        for u in range(2):
            slot = qring.take(S, lanes)
            wait(S)
            turn = bass.ds(2 * i + u, 1)
            src = [qstack.rearrange("b (g a) r t -> (b g) r a t", a=HG)[turn].rearrange("x r a t -> (x r) a t"),
                   kstack.rearrange("b g r t -> (b g) r t")[turn].rearrange("x r t -> (x r) t"),
                   vstack.rearrange("b g p v -> (b g) p v")[turn].rearrange("x p v -> (x p) v"),
                   maxima[turn].rearrange("x m t -> (x m) t")]
            dst = [qs[0:TERMS * AD, slot, :, :], ks[0:TERMS * AD, slot, :], vs[:, slot, :, :].rearrange("p q v -> p (q v)"),
                   qs[MROW:MROW + 3, slot, :, :].rearrange("p a t -> p (a t)")]
            fetched.append((slot, [a.started(slot, S.dma_start(d_, s_)) for a, d_, s_ in zip(arr, dst, src)]))
        later = []

        def weigh(task):
            slot, blk, off, pslot, a, th, nblk = task
            if blk == 0:
                sring.take(E, lanes)
            bank, bslot = sums[0], 0
            wait(E, a)
            for h in range(HG):
                p = E.matmul(bank[VW * h:VW * h + VW, off:TILE], vs[:, slot, blk, :], prob[:, pslot, h, off:TILE],
                             start=blk == 0, stop=True, skip_group_check=True)
            p = pe(p)
            pring.release(pslot, p)
            if blk == nblk - 1:
                wait(V, p)
                u = fetched.index(next(f for f in fetched if f[0] == slot))
                d = dve(V.tensor_copy(y[:, bass.ds((2 * i + u) * T + th * TILE, TILE)], bank[:, :]))
                sring.release(bslot, d)
            return p

        for u in range(2):
            slot, landed = fetched[u]
            for a_, l in zip(arr, landed):
                a_.wait(E, l)
            for th in range(2):
                nblk = 4 * (th + 1)
                for blk in range(nblk):
                    off = max(0, blk * CH - th * TILE)
                    pslot = None
                    for h in range(HG):
                        t = ring.take(E, lanes)
                        rslot = ring.slot
                        wait(E)
                        p = E.matmul(t[:, off:TILE], ks[0:SROWS, slot, blk * CH:(blk + 1) * CH],
                                     qs[0:SROWS, slot, h, th * TILE + off:(th + 1) * TILE], start=True, stop=True)
                        if blk >= 4 * th:
                            p = E.matmul(t[:, off:off + CH], k.bf["ident"], k.bf["earlier_t"],
                                         start=False, stop=True, skip_group_check=True)
                        p = pe(p)
                        if h == 0:
                            pring.take(A, lanes)
                            pslot = pring.slot
                        wait(A, p)
                        a = act(A.activation(prob[:, pslot, h, off:TILE], t[:, off:TILE], ACT.Exp, scale=SCALE))
                        ring.release(rslot, a)
                        if h == 1 and later:
                            last = weigh(later.pop())
                        yield
                    later.append((slot, blk, off, pslot, a, th, nblk))
            last = weigh(later.pop())
            qring.release(slot, last)
    return task


def attention_out(k, w, y, x, z, result):
    nc = k.nc
    V, A, E, S, G = nc.vector, nc.scalar, nc.tensor, nc.sync, nc.gpsimd
    cols = NB * NG * T
    sums = nc.dram_tensor("sums", (HG, cols), F32, kind="Internal").ap()
    inverse = nc.dram_tensor("inverse", (HG, cols), F32, kind="Internal").ap()
    with ExitStack() as c:
        dense = k.sb("ao_dense", [P, HG * cols // P], ctx=c)
        inv = k.sb("ao_inv", [P, 2, NG, T], ctx=c)
        bank = [k.ps(f"ao_bank{n}", [P, TILE], c) for n in range(4)]
        moved, inverted, stored = k.sem("ao_moved"), k.sem("ao_inverted"), k.sem("ao_stored")
        for h in range(HG):
            S.dma_start(sums[h:h + 1, :], y[VW * h + AD:VW * h + AD + 1, :]).then_inc(moved, 16)
        S.wait_ge(moved, 16 * HG)
        flat = lambda t: t.rearrange("h (p n) -> (h p) n", p=P // HG)
        S.dma_start(dense[:, :], flat(sums)).then_inc(moved, 16)
        V.wait_ge(moved, 16 * (HG + 1))
        V.reciprocal(dense[:, :], dense[:, :]).then_inc(inverted, 1)
        S.wait_ge(inverted, 1)
        S.dma_start(flat(inverse), dense[:, :]).then_inc(moved, 16)
        S.wait_ge(moved, 16 * (HG + 2))
        task = Task(k, "ao")

        @task.body
        def _(i, pe, dve, act, pool, sp):
            lanes = task.lanes
            ring = Ring(k, "ao_ring", bank)
            iring, iarr = Ring(k, "ao_iring", [0, 1]), Arrivals(k, "ao_iarr", [0, 1], sp)
            got = []
            for u in range(2):
                slot = iring.take(S, lanes)
                wait(S)
                src = inverse[:, bass.ds((2 * i + u) * NG * T, NG * T)].unsqueeze(1).broadcast_to([HG, VW, NG * T])
                got.append((slot, iarr.started(slot, S.dma_start(inv[:, slot, :, :].rearrange("p g t -> p (g t)"), src))))
            for u in range(2):
                slot, landed = got[u]
                iarr.wait(V, landed)
                yb = [y[:, bass.ds(((2 * i + u) * NG + g) * T, T)] for g in range(NG)]
                d = []
                for g in range(NG):
                    wait(V)
                    d.append(dve(V.tensor_tensor(inv[:, slot, g, :], inv[:, slot, g, :], yb[g], ALU.mult)))
                for half in range(2):
                    t = ring.take(E, lanes)
                    rslot = ring.slot
                    for g in range(NG):
                        wait(E, d[g])
                        p = E.matmul(t[:, :], w(f"wproj{g}"), inv[:, slot, g, half * TILE:(half + 1) * TILE], start=g == 0, stop=g == NG - 1)
                    p = pe(p)
                    cols = bass.ds((2 * (2 * i + u) + half) * TILE, TILE)
                    xz = pool(G.tensor_tensor(x[:, cols], x[:, cols], z[:, cols], ALU.add))
                    wait(V, p, xz)
                    v = dve(V.tensor_tensor(x[:, cols], t[:, :], x[:, cols], ALU.add))
                    ring.release(rslot, v)
                    wait(A, v)
                    A.dma_start(result[:, cols], x[:, cols]).then_inc(stored, 16)
                iring.release(slot, p)
            task.ends.append(iarr.end)
            yield

        run(k, NB // 2, task)
        for e in k.all_engines():
            e.wait_ge(stored, 16 * NT)


ME, MF = 8, 256


def moe1(k, w, w13, w2, share, z, zn, eps, company):
    nc = k.nc
    V, A, E, S, G = nc.vector, nc.scalar, nc.tensor, nc.sync, nc.gpsimd
    nt = N // CH
    for loop, along in enumerate(company):
        tag = f"m1{loop}"
        normalise(k, f"{tag}n", lambda t: z[:, bass.ds(t * TILE, TILE)], lambda t: zn[:, bass.ds(t * TILE, TILE)],
                  w, w("mean128", 0, 32), eps, gain=w("normw"))
        with ExitStack() as c2:
            bank = k.ps(f"{tag}_router", [P, nt * ME], c2)
            t = {n: k.sb(f"{tag}_{n}", [P, nt * ME], ctx=c2) for n in ("eq", "one", "two", "rest", "soft", "logits")}
            t |= {n: k.sb(f"{tag}_{n}", [P, nt], ctx=c2) for n in ("peak", "peak2", "place", "sum")}
            lane = {n: Lane(k, e, f"{tag}r_{n}", 0, 1) for n, e in (("dve", V), ("act", A), ("pe", E))}
            for l in lane.values():
                l.engine.sem_inc(l.sem, l.per)
            for n in range(nt):
                p = E.matmul(bank[:, n * ME:(n + 1) * ME], zn[:, n * CH:(n + 1) * CH], w("router"), start=True, stop=True)
            p = lane["pe"](p)
            wait(A, p)
            a = lane["act"](A.activation(t["logits"][:, :], bank[:, :], ACT.Copy))
            wait(V, a)
            v, wide, inv = finish(top2(k, w, V, A, lane["dve"], lane["act"], t["logits"][:, :].rearrange("p (g e) -> p g e", e=ME), nt, ME, t, False))
            d = lane["dve"](V.scalar_tensor_tensor(share[:, :].rearrange("p (g e) -> p g e", e=ME), v("one"), 1.0 if loop == 0 else 0.5,
                                                   wide("sum"), ALU.mult, ALU.mult))
            for l in lane.values():
                k.seen[l.name] = l.pos
            for e in k.all_engines():
                wait(e, d)
        with ExitStack() as c2:
            beside = along(c2)
            s2 = lambda name, *shape: k.sb(f"{tag}_{name}", [P, *shape], ctx=c2)
            up = [k.ps(f"{tag}_up{n}", [P, TILE], c2) for n in range(3)]
            down = [k.ps(f"{tag}_down", [P, NC, HID], c2)]
            silu = [s2(f"silu{n}", TILE) for n in range(3)]
            hid = [s2(f"hid{n}", TILE) for n in range(4)]
            mixed = [s2(f"mixed{n}", HID) for n in range(NC)]
            task = Task(k, tag)

            @task.body
            def _(i, pe, dve, act, pool, sp):
                lanes = task.lanes
                upring, dring = Ring(k, f"{tag}_upr", up), Ring(k, f"{tag}_dr", down)
                sring, hring = Ring(k, f"{tag}_sr", silu), Ring(k, f"{tag}_hr", hid)
                zt = zn[:, bass.ds(i * TILE, TILE)]
                added = [None] * NC

                def ups(e, f):
                    ab = []
                    for a_ in range(2):
                        t_ = upring.take(E, lanes)
                        uslot = upring.slot
                        wait(E)
                        ab.append((t_, uslot, pe(E.matmul(t_[:, :], w13[:, e, a_, f * P:(f + 1) * P], zt, start=True, stop=True))))
                        yield
                    (ta, sa, pa), (tb, sb_, pb) = ab
                    s_ = sring.take(A, lanes)
                    sslot = sring.slot
                    wait(A, pa)
                    if loop == 0:
                        a_ = act(A.activation(s_[:, :], ta[:, :], ACT.Silu))
                        upring.release(sa, a_)
                    else:
                        a_ = act(A.activation(s_[:, :], ta[:, :], ACT.Tanh, scale=0.5))
                        wait(V, a_)
                        a_ = dve(V.scalar_tensor_tensor(s_[:, :], s_[:, :], 1.0, ta[:, :], ALU.add, ALU.mult))
                        upring.release(sa, a_)
                    if loop == 0:
                        h_ = hring.take(A, lanes)
                        hslot = hring.slot
                        wait(A, pb)
                        c_ = act(A.activation(h_[:, :], tb[:, :], ACT.Copy))
                        upring.release(sb_, c_)
                        wait(G, a_, c_)
                        d_ = pool(G.tensor_tensor(h_[:, :], s_[:, :], h_[:, :], ALU.mult))
                    else:
                        h_ = hring.take(V, lanes)
                        hslot = hring.slot
                        wait(V, a_, pb)
                        d_ = dve(V.tensor_tensor(h_[:, :], s_[:, :], tb[:, :], ALU.mult))
                        upring.release(sb_, d_)
                    sring.release(sslot, d_)
                    return h_, hslot, d_

                def downs(e, hs):
                    t_ = dring.take(E, lanes)
                    dslot = dring.slot
                    wait(E, *[h_[2] for h_ in hs])
                    for n in range(NC):
                        if n == 2:
                            yield
                        for f in range(2):
                            p_ = E.matmul(t_[:, n, :], hs[f][0][:, n * CH:(n + 1) * CH], w2[:, e, f, :], start=f == 0, stop=f == 1)
                    p_ = pe(p_)
                    for h_ in hs:
                        hring.release(h_[1], p_)
                    wait(V, p_)
                    for n in range(NC):
                        g = share[:, bass.ds((i * NC + n) * ME + e, 1)]
                        if e == 0:
                            wait(V, pe.last("turn"))
                            d_ = added[n] = dve(V.tensor_scalar(mixed[n][:, :], t_[:, n, :], g, None, ALU.mult))
                        else:
                            wait(V, added[n])
                            d_ = added[n] = dve(V.scalar_tensor_tensor(mixed[n][:, :], t_[:, n, :], g, mixed[n][:, :], ALU.mult, ALU.add))
                    dring.release(dslot, d_)

                later = None
                for e in range(ME):
                    hs = [(yield from ups(e, 0))]
                    if later:
                        yield from downs(*later)
                    hs.append((yield from ups(e, 1)))
                    if loop == 1:
                        yield
                    later = (e, hs)
                yield from downs(*later)
                yield
                back = dring.take(E, lanes)
                bslot = dring.slot
                wait(E, *added)
                for n in range(NC):
                    p = E.transpose(back[:, n, :], mixed[n][:, :], w("ident"))
                p = pe(p, "turn")
                zc = z[:, bass.ds(i * TILE, TILE)]
                wait(V, p)
                dring.release(bslot, dve(V.tensor_tensor(zc, back[:, :, :].rearrange("p n t -> p (n t)"), zc, ALU.add)))
                yield
            run(k, NT, task, beside)


def program(nc, dram, counts):
    with ExitStack() as ctx:
        k = Kit(nc, ctx, counts, dram)
        x = k.sb("x", [P, N])
        consts = {"shared": k.sb("shared", list(dram["shared"].shape))}
        landed = k.sem("landed")

        def w(name, a=0, b=None):
            array, off, width = COLS[name]
            return consts[array][:, off + a:off + (width if b is None else b)]

        k.w_at = lambda name, i: consts["const0"][:, bass.ds(COLS[name][1] + i, 1)]
        zero = k.sem("zero")
        eps = k.sb("eps", [P, 1])
        nc.vector.memset(eps[:, :], 1e-5).then_inc(zero, 1)
        k.bf = {}

        def in_bf16(name):
            t = k.sb(f"bf_{name}", [P, P], BF16)
            nc.vector.tensor_copy(t[:, :], w(name)).then_inc(zero, 1)
            k.bf[name] = t[:, :]

        bf_ident = k.sb("bf_ident", [P, P], BF16)
        with ExitStack() as c0:
            consts["const0"] = k.sb("const0", list(dram["const0"].shape), ctx=c0)
            n = load(k, landed, 0, (x[:, :], dram["x"]), (consts["shared"][:, :], dram["shared"]), (consts["const0"][:, :], dram["const0"]))
            nc.vector.wait_ge(landed, n)
            nc.vector.tensor_copy(bf_ident[:, :], w("ident")).then_inc(zero, 1)
            k.bf["ident"] = bf_ident[:, :]
            xn = k.sb("xn", [P, (NT + 1) * PITCH], ctx=c0)
            nc.vector.memset(xn[:, 0:1], 0.0).then_inc(zero, 1)
            for e in k.all_engines():
                e.wait_ge(landed, n)
                e.wait_ge(zero, 3)

            def last_token(t, dve, out):
                wait(nc.vector, out)
                dve(nc.vector.tensor_scalar(xn[:, bass.ds((t + 1) * PITCH, 1)], xn[:, bass.ds(t * PITCH + TILE, 1)], k.w_at("follows", t), None, ALU.mult))

            w1s = k.sb("w1s", [TERMS * FD, FE * FI], BF16, ctx=c0)
            c1 = c0.enter_context(ExitStack())
            weights_ready = moe0_weights(k, c1, w, w1s)
            normalise(k, "ln0", lambda t: x[:, bass.ds(t * TILE, TILE)], lambda t: xn[:, bass.ds(t * PITCH + 1, TILE)],
                      w, w("mean128", 0, 32), eps, w("mean128"), extra=last_token)
            stack = nc.dram_tensor("stack", (NT, FH, TERMS * FD, TILE), BF16, kind="Internal").ap()
            shares = nc.dram_tensor("shares", (NT, FH * FE, TILE), F32, kind="Internal").ap()
            with c1:
                run(k, NT // 2, *[moe0_prepare(k, c1, w, xn, stack, shares, f"mp{n}", n) for n in range(2)])
            weights_ready()
            gate = k.sb("rw_gate", [P, N], ctx=c0)
            out = xn
            with ExitStack() as c1:
                rw = recurrence(k, c1, w, xn, out, gate)
                run(k, NT // 2, moe0(k, c1, w, w1s, stack, shares, x), rw)
            normalise(k, "gn", lambda t: out[:, bass.ds(t * PITCH + 1, TILE)], lambda t: out[:, bass.ds(t * PITCH + 1, TILE)],
                      w, w("mean32").rearrange("p (n f) -> p n f", f=4)[:, :, 0], eps, w("mean32"))
            recurrence_out(k, w, out, gate, x)
        z, zn = k.sb("z", [P, N]), k.sb("zn", [P, N])
        tile = lambda buf: lambda t: buf[:, bass.ds(t * TILE, TILE)]
        consts["const1"] = k.sb("const1", list(dram["const1"].shape))
        w13, w2 = k.sb("w13", [P, ME, 2, MF]), k.sb("w2", [P, ME, 2, HID])
        n = load(k, landed, n, (consts["const1"][:, :], dram["const1"]),
                 (w13[:, :, :, :].rearrange("p e a f -> p (e a f)"), dram["w13"]), (w2[:, :, :, :].rearrange("p e a f -> p (e a f)"), dram["w2b"]))
        normalise(k, "ln1", tile(x), tile(z), w, w("mean128", 0, 32), eps, w("mean128"))
        for e in k.all_engines():
            e.wait_ge(landed, n)
        for name in ("later_s", "earlier_t"):
            in_bf16(name)
        with ExitStack() as c1:
            scratch = lambda name, shape, dt: nc.dram_tensor(name, shape, dt, kind="Internal").ap()
            qstack = scratch("qstack", (NB, AH, TERMS * AD, T), BF16)
            kstack = scratch("kstack", (NB, NG, TERMS * AD, T), BF16)
            vstack = scratch("vstack", (NB, NG, P, QB * VW), F32)
            maxima = scratch("maxima", (NB * NG, 3, HG * T), BF16)
            y = k.sb("y", [P, NB * NG * T], ctx=c1)
            share = k.sb("m1_share", [P, N // CH * ME], ctx=c1)
            c2 = c1.enter_context(ExitStack())
            with ExitStack() as cbank:
                prepare = [attention_prepare(k, c2, cbank, w, z, qstack, kstack, vstack, half) for half in range(2)]
                run(k, NB, *prepare)

            def first(c):
                for task in prepare:
                    task.drained()
                c2.close()
                return attention_max(k, c, w, qstack, kstack, maxima)

            nc.vector.memset(eps[:, :], 1e-6).then_inc(zero, 1)
            for e in k.all_engines():
                e.wait_ge(zero, 6)
            moe1(k, w, w13, w2, share, z, zn, eps, (first, lambda c: attention_sum(k, c, w, qstack, kstack, vstack, maxima, y)))
            attention_out(k, w, y, x, z, dram["out"])
        return k.seen


COLS = {}


def pack(array, parts):
    import numpy as np
    off, out = 0, []
    for name, a in parts:
        a = np.asarray(a)
        if a.shape[0] < P:
            a = np.concatenate([a, np.zeros((P - a.shape[0], a.shape[1]), a.dtype)])
        COLS[name] = (array, off, a.shape[1])
        off += a.shape[1]
        out.append(a)
    return np.ascontiguousarray(np.concatenate(out, axis=1))


def arrays(**inputs):
    import numpy as np
    g = {n: np.asarray(a) for n, a in inputs.items()}
    a = {n[8:]: v for n, v in g.items() if n.startswith("L0_attn_")}
    f32 = np.float32
    col = lambda v: v.reshape(-1, 1)
    pad = lambda m, cols: np.concatenate([m, np.zeros((m.shape[0], cols - m.shape[1]), m.dtype)], axis=1)
    part = np.arange(P)
    x0t = a["W_x0"].T
    x2 = a["W_x2"].reshape(HID, 5, 32)
    shared = [("mean128", np.full((P, P), 1 / P, f32)),
             ("spread", np.concatenate([(part[:, None] == 32 * g + 8 * (part // 32)).astype(f32) for g in range(4)], axis=1)),
             ("ident", np.eye(P, dtype=f32)),
             ("descending", np.tile(np.arange(16, 0, -1).astype(f32), (P, 1)))]
    parts = [
             ("mean32", np.kron(np.eye(4, dtype=f32), np.full((32, 32), 1 / 32, f32))),
             ("follows", np.tile(np.array([1, 0], f32), (P, NT // 2))),
             ("carries", np.tile(np.array([0, 1], f32), (P, NT // 4))),
             ("headmask", ((part[:, None] % KD) // DK == np.arange(NH)).astype(f32)),
             ("statemask", ((part[:, None] % KD) // DK == part // DV).astype(f32)),
             ("eye32", (part[:, None] % SB == np.arange(SB)).astype(f32))]
    s32 = part[:, None] % SB
    for h in LOW:
        right = np.array([t for t in range(SB) if (t // h) % 2])
        parts.append((f"mask{h}", ((s32 // (2 * h) == right // (2 * h)) & ((s32 // h) % 2 == 0)).astype(f32)))
    parts += [("mu0", col(a["mu0"])), ("wx00", x0t[:, :P]), ("wx01", pad(x0t[:, P:], P)), ("xbias", a["x_bias"].T)]
    for i in range(5):
        m = np.zeros((P, P), f32)
        m[32 * (i % 4):32 * (i % 4) + 32] = x2[:, i, :].T
        parts.append((f"wx2{i}", m))
    parts += [("wr", a["W_r"].T), ("wk", a["W_k"].T), ("ww1", pad(a["W_w1"].T, P)), ("ww2", a["W_w2"].T),
              ("bw2", np.tile(col(a["b_w2"]), (2, 1))), ("bonus", np.tile(col(a["bonus"].reshape(-1)), (2, 1))),
              ("wv", a["W_v"].T), ("wg", a["W_g"].T), ("wo", a["W_o"].T), ("gnw", col(a["gn_weight"])), ("gnb", col(a["gn_bias"]))]
    g0 = {n[7:]: v for n, v in g.items() if n.startswith("L0_ffn_")}
    emb = np.zeros((P, P), f32)
    for n in range(FH):
        emb[n * FD:(n + 1) * FD, n * FE:(n + 1) * FE] = g0["expert_emb"]
    parts += [("wm", g0["Wm"]), ("bm", col(g0["bm"])), ("emb", emb),
              ("wo0", np.tile(g0["Wo"].reshape(FH, 1, FD, HID), (1, P // FD, 1, 1)).reshape(FH, P, HID).transpose(1, 0, 2).reshape(P, -1)),
              ("b1", g0["b1"].reshape(EP, P).T), ("b2", g0["b2"].reshape(2, P).T), ("bo", col(g0["bo"]))]
    for n in range(3):
        parts.append((f"rows{n}", col(np.repeat(np.array([p == n for p in WEIGHT_PARTS], f32), FD))))
    w2 = np.zeros((EP, 2, FI, 2, FD), f32)
    for n in range(2):
        w2[:, n, :, n, :] = g0["W2"].reshape(EP, 2, FI, FD)[:, n]
    parts.append(("w2", np.transpose(w2.reshape(EP, P, 2 * FD), (1, 0, 2)).reshape(P, EP * 2 * FD)))
    w1 = np.ascontiguousarray(np.tile(np.transpose(g0["W1"], (1, 0, 2)).reshape(FD, FE * FI), (TERMS, 1)))
    a1 = {n[8:]: v for n, v in g.items() if n.startswith("L1_attn_")}
    f1 = {n[7:]: v for n, v in g.items() if n.startswith("L1_ffn_")}
    later = np.where(part[None, :] > part[:, None], f32(-1e30), f32(0))
    proj = a1["Wc_proj"].reshape(NG, HG, AD, HID)
    const0 = pack("const0", parts)
    parts = [("wdown", pad(a1["Wc_down"], P)), ("wqup", a1["Wq_up"]), ("wkup", pad(a1["Wkv_up"][:, :AD], 32)),
              ("wvup", pad(a1["Wkv_up"][:, AD:], VW)), ("later_s", later), ("earlier_t", later.T),
              ("sumcolumn", np.tile((np.arange(VW) == AD).astype(f32), (P, 1))),
              ("normw", col(f1["norm_w"])), ("router", f1["router_w"])]
    for n in range(NG):
        m = np.zeros((HG, VW, HID), f32)
        m[:, :AD] = proj[n]
        parts.append((f"wproj{n}", m.reshape(P, HID)))
    w13 = np.transpose(np.stack([f1["w1"], f1["w3"]], axis=1), (2, 0, 1, 3)).reshape(HID, -1)
    w2b = np.transpose(f1["w2"].reshape(ME, 2, P, HID), (2, 0, 1, 3)).reshape(P, -1)
    return {"w13": np.ascontiguousarray(w13), "w2b": np.ascontiguousarray(w2b), "w1": w1, "x": np.ascontiguousarray(a["hidden_states"].reshape(N, HID).T), "shared": pack("shared", shared), "const0": const0, "const1": pack("const1", parts)}


def make(bacc, ins):
    counts = {}
    for _ in range(2):
        nc = bacc("TRN2", target_bir_lowering=False, num_devices=1)
        dram = {n: nc.dram_tensor(f"in_{n}", v.shape, mybir.dt.from_np(v.dtype), kind="ExternalInput").ap() for n, v in ins.items()}
        dram["out"] = nc.dram_tensor("out_0", (P, N), F32, kind="ExternalOutput").ap()
        counts = program(nc, dram, counts)
    return nc


def kernel(**inputs):
    import concourse.bacc as bacc
    import numpy as np
    from concourse.bass_utils import run_bass_kernel_spmd

    ins = arrays(**inputs)
    nc = make(bacc.Bacc, ins)
    r = run_bass_kernel_spmd(nc, [{f"in_{n}": a for n, a in ins.items()}], core_ids=[0])
    return np.ascontiguousarray(r.results[0]["out_0"].T).reshape(NB, T, HID)
```
